# Optimizing a Trainium2 kernel written in Bass

```python
import numpy as np
import jax
import jax.numpy as jnp

def _softmax(x, axis=-1):
    return jax.nn.softmax(x, axis=axis)

def _gelu(x):
    return jax.nn.gelu(x, approximate=True)

def _silu(x):
    return jax.nn.silu(x)

def _sigmoid(x):
    return jax.nn.sigmoid(x)

def _layernorm(x, axis=-1, eps=1e-05):
    m = jnp.mean(x, axis=axis, keepdims=True)
    v = jnp.var(x, axis=axis, keepdims=True)
    return (x - m) / jnp.sqrt(v + eps)

def _scatter_add(tgt, idx, src, axis=0):
    return tgt.at[idx].add(src)

def _segment_sum(src, seg, n):
    return jax.ops.segment_sum(src, seg, n)
kernel_name = 'mk_gnn_preln_d2_gnn_r32_a7ceda'

def setup_inputs(seed: int=0):
    np.random.seed(seed)
    _w = jnp.asarray

    def _rec_inputs():
        import jax
        import jax.numpy as jnp
        _gk = jax.random.key(seed)
        x = -0.0002117 + 1 * jax.random.normal(jax.random.fold_in(_gk, 1), (3125, 256), jnp.float32)
        _s = jax.random.randint(jax.random.fold_in(_gk, 2), (25000,), 0, 3125, jnp.int32)
        _d = jax.random.randint(jax.random.fold_in(_gk, 3), (25000,), 0, 3125, jnp.int32)
        _loop = jnp.arange(3125, dtype=jnp.int32)
        src = jnp.concatenate([_s, _d, _loop])
        dst = jnp.concatenate([_d, _s, _loop])
        _o = jnp.argsort(dst, stable=True)
        src = src[_o]
        dst = dst[_o]
        edge_weight = jax.random.uniform(jax.random.fold_in(_gk, 12), (53125,), jnp.float32, 0.0, 1)
        return (x, src, dst, edge_weight)
    x, src, dst, edge_weight = _rec_inputs()

    def _L0_gnn_setup():
        import jax, jax.numpy as jnp
        import numpy as np
        N_NODES = 3125
        N_EDGES = 100000
        C = 256
        key = jax.random.key(seed)
        k1, k2, k3, k4 = jax.random.split(key, 4)
        x = jax.random.normal(k1, (N_NODES, C), dtype=jnp.float32)
        edge_weight = jax.random.uniform(k2, (N_EDGES,), dtype=jnp.float32)
        row = jax.random.randint(k3, (N_EDGES,), 0, N_NODES)
        col = jax.random.randint(k4, (N_EDGES,), 0, N_NODES)
        edge_index = jnp.stack([row, col]).astype(jnp.int64)
        return {'x': x, 'edge_weight': edge_weight, 'edge_index': edge_index}
    _L0_gnn_all = _L0_gnn_setup()
    _L0_gnn_in = {k: v for k, v in _L0_gnn_all.items() if k in ()}
    del _L0_gnn_all

    def _L1_gnn_setup():
        import jax, jax.numpy as jnp
        import numpy as np
        ALPHA = 0.2
        LN_EPS = 1e-05

        def _gat_layer(x, src, dst, W, b, a, g, beta, N, concat):
            h = x @ W.T + b
            d = W.shape[0]
            s_src = h @ a[:d]
            s_dst = h @ a[d:]
            score = s_src[src] + s_dst[dst]
            e = jnp.exp(-jax.nn.leaky_relu(score, ALPHA))
            h_prime = jax.ops.segment_sum(e[:, None] * h[dst], src, num_segments=N)
            mu = jnp.mean(h_prime, axis=-1, keepdims=True)
            var = jnp.var(h_prime, axis=-1, keepdims=True)
            h_prime = (h_prime - mu) * jax.lax.rsqrt(var + LN_EPS) * g + beta
            return jax.nn.elu(h_prime) if concat else h_prime
        key = jax.random.key(seed)
        ks = jax.random.split(key, 13)
        N, E, F, D, H = (50000, 25000, 256, 64, 8)
        S = 0.02
        inp = {'embeds': jax.random.normal(ks[0], (N, F), dtype=jnp.float32), 'W_heads': jax.random.normal(ks[1], (H, D, F), dtype=jnp.float32) * S, 'b_heads': jax.random.normal(ks[2], (H, D), dtype=jnp.float32) * S, 'a_heads': jax.random.normal(ks[3], (H, 2 * D), dtype=jnp.float32) * S, 'g_heads': jnp.ones((H, D), dtype=jnp.float32), 'beta_heads': jnp.zeros((H, D), dtype=jnp.float32), 'W_out': jax.random.normal(ks[4], (F, D * H), dtype=jnp.float32) * S, 'b_out': jax.random.normal(ks[5], (F,), dtype=jnp.float32) * S, 'a_out': jax.random.normal(ks[6], (2 * F,), dtype=jnp.float32) * S, 'g_out': jnp.ones((F,), dtype=jnp.float32), 'beta_out': jnp.zeros((F,), dtype=jnp.float32), 'edge_index': jax.random.randint(ks[7], (2, E), 0, N, dtype=jnp.int32)}
        return inp
    _L1_gnn_all = _L1_gnn_setup()
    _L1_gnn_in = {k: v for k, v in _L1_gnn_all.items() if k in ('W_heads', 'b_heads', 'a_heads', 'g_heads', 'beta_heads', 'W_out', 'b_out', 'a_out', 'g_out', 'beta_out')}
    del _L1_gnn_all
    return {'x': x, 'src': src, 'dst': dst, 'edge_weight': edge_weight, 'L1_gnn_W_heads': _L1_gnn_in['W_heads'], 'L1_gnn_b_heads': _L1_gnn_in['b_heads'], 'L1_gnn_a_heads': _L1_gnn_in['a_heads'], 'L1_gnn_g_heads': _L1_gnn_in['g_heads'], 'L1_gnn_beta_heads': _L1_gnn_in['beta_heads'], 'L1_gnn_W_out': _L1_gnn_in['W_out'], 'L1_gnn_b_out': _L1_gnn_in['b_out'], 'L1_gnn_a_out': _L1_gnn_in['a_out'], 'L1_gnn_g_out': _L1_gnn_in['g_out'], 'L1_gnn_beta_out': _L1_gnn_in['beta_out']}

def reference(x, src, dst, edge_weight, L1_gnn_W_heads, L1_gnn_b_heads, L1_gnn_a_heads, L1_gnn_g_heads, L1_gnn_beta_heads, L1_gnn_W_out, L1_gnn_b_out, L1_gnn_a_out, L1_gnn_g_out, L1_gnn_beta_out):
    import jax
    import jax.numpy as jnp

    def _L0_gnn_ref(x, edge_weight, edge_index):
        import jax, jax.numpy as jnp
        import numpy as np
        N_NODES = 3125
        N_EDGES = 100000
        C = 256
        n = x.shape[0]
        c_half = x.shape[-1] // 2
        row, col = (edge_index[0], edge_index[1])
        ones = jnp.ones(edge_index.shape[1], dtype=x.dtype)
        deg_row = jax.ops.segment_sum(ones, row, num_segments=n)
        deg_col = jax.ops.segment_sum(ones, col, num_segments=n)
        w = edge_weight[:, None]
        msg_fwd = w * x[col, :c_half]
        x_fwd = jax.ops.segment_sum(msg_fwd, row, num_segments=n)
        x_fwd = x_fwd / jnp.clip(deg_row, 1.0)[:, None]
        msg_bwd = w * x[row, c_half:]
        x_bwd = jax.ops.segment_sum(msg_bwd, col, num_segments=n)
        x_bwd = x_bwd / jnp.clip(deg_col, 1.0)[:, None]
        return jnp.concatenate([x_fwd, x_bwd], axis=-1)

    def _L1_gnn_ref(embeds, W_heads, b_heads, a_heads, g_heads, beta_heads, W_out, b_out, a_out, g_out, beta_out, edge_index):
        import jax, jax.numpy as jnp
        import numpy as np
        ALPHA = 0.2
        LN_EPS = 1e-05

        def _gat_layer(x, src, dst, W, b, a, g, beta, N, concat):
            h = x @ W.T + b
            d = W.shape[0]
            s_src = h @ a[:d]
            s_dst = h @ a[d:]
            score = s_src[src] + s_dst[dst]
            e = jnp.exp(-jax.nn.leaky_relu(score, ALPHA))
            h_prime = jax.ops.segment_sum(e[:, None] * h[dst], src, num_segments=N)
            mu = jnp.mean(h_prime, axis=-1, keepdims=True)
            var = jnp.var(h_prime, axis=-1, keepdims=True)
            h_prime = (h_prime - mu) * jax.lax.rsqrt(var + LN_EPS) * g + beta
            return jax.nn.elu(h_prime) if concat else h_prime
        N = embeds.shape[0]
        src, dst = (edge_index[0], edge_index[1])
        H = W_heads.shape[0]
        heads = [_gat_layer(embeds, src, dst, W_heads[i], b_heads[i], a_heads[i], g_heads[i], beta_heads[i], N, concat=True) for i in range(H)]
        x = jnp.concatenate(heads, axis=1)
        out = _gat_layer(x, src, dst, W_out, b_out, a_out, g_out, beta_out, N, concat=False)
        return jax.nn.elu(out)
    edge_index = jnp.stack([src, dst])
    h = jnp.maximum(_layernorm(x, axis=-1), 0.0)
    x = x + _L0_gnn_ref(h, edge_weight, edge_index)
    h = jnp.maximum(_layernorm(x, axis=-1), 0.0)
    x = x + _L1_gnn_ref(h, L1_gnn_W_heads, L1_gnn_b_heads, L1_gnn_a_heads, L1_gnn_g_heads, L1_gnn_beta_heads, L1_gnn_W_out, L1_gnn_b_out, L1_gnn_a_out, L1_gnn_g_out, L1_gnn_beta_out, edge_index)
    return x

_drawn_inputs = setup_inputs


def setup_inputs(seed=0):
    import zlib

    import numpy as np

    out = dict(_drawn_inputs(seed))
    spreads = {'L1_gnn_g_heads': (1.0, 0.2),
     'L1_gnn_beta_heads': (0.0, 0.1),
     'L1_gnn_g_out': (1.0, 0.2),
     'L1_gnn_beta_out': (0.0, 0.1)}
    factors = {'L1_gnn_a_heads': 8.0, 'L1_gnn_a_out': 22.837}
    for name, (base, spread) in spreads.items():
        noise = np.random.default_rng([zlib.crc32(name.encode()), seed]).standard_normal(out[name].shape)
        drawn = base * np.exp(spread * noise) if base else spread * noise
        out[name] = jnp.asarray(drawn.astype(out[name].dtype))
    for name, factor in factors.items():
        out[name] = (out[name] * factor).astype(out[name].dtype)
    return out
```

```python
import concourse.bass as bass
from concourse import mybir
from contextlib import ExitStack

F32 = mybir.dt.float32
I32 = mybir.dt.int32
BF16 = mybir.dt.bfloat16
FP16 = mybir.dt.float16
U16 = mybir.dt.uint16
ALU = mybir.AluOpType
ACT = mybir.ActivationFunctionType
AX = mybir.AxisListType

P = 128
N = 3125
C = 256
HALF = C // 2
E = 53125
HEADS, D = 8, 64
HD = HEADS * D
T = -(-N // P)
LAST = N - (T - 1) * P
COLS = -(-E // P)
TAIL = E - (P - 1) * COLS
GP = 2
GROUPS = (E + T * (GP * P - 1)) // (GP * P)
CHUNKS = GROUPS * GP
QUAD = 4
QUADS = CHUNKS // QUAD
CHP = CHUNKS + QUAD
GPAD = CHP // GP
SLOTS = 8
ROUNDS = CHUNKS // SLOTS
SORT_ROUNDS = COLS // SLOTS
RING = 4
W1 = HD + HEADS
W2 = C + 1
NO_POS = 65537.0
EPS = 1e-5
ALPHA = 0.2
assert CHUNKS % SLOTS == 0 and COLS % SLOTS == 0 and CHP <= 512 and QUADS % 2 == 0


def build(nc, x, src, dst, edge_weight, W_heads, b_heads, a_heads, g_heads, beta_heads,
          W_out, b_out, a_out, g_out, beta_out, out):
    ctx = ExitStack()
    with ctx:
        def sb(name, shape, dt=F32):
            return ctx.enter_context(nc.sbuf_tensor(name, shape, dt))

        def sem(name):
            return ctx.enter_context(nc.semaphore(name))

        ctx.enter_context(nc.allow_non_contiguous_dma(reason="small weight vectors"))
        bank = [ctx.enter_context(nc.psum_tensor(f"bank{i}", [P, 512], F32)) for i in range(8)]

        table_a = nc.dram_tensor("table_a", (T * P, HALF), F32, kind="Internal").ap()
        table_b = nc.dram_tensor("table_b", (T * P, HALF), F32, kind="Internal").ap()
        table_1 = nc.dram_tensor("table_1", (T * P, W1), F32, kind="Internal").ap()
        table_2 = nc.dram_tensor("table_2", (T * P, W2), F32, kind="Internal").ap()

        iota_f = sb("iota_f", [P, 512])
        iota_lane = sb("iota_lane", [P, P], BF16)
        iota_chunk = sb("iota_chunk", [P, CHP], FP16)
        row_i = sb("row_i", [P, 1], I32)
        row_f = sb("row_f", [P, 1])
        ident = sb("ident", [P, P])
        before = sb("before", [P, P])
        ones = sb("ones", [P, COLS])
        zero_lhs = sb("zero_lhs", [P, P], BF16)
        eps = sb("eps", [P, 1])

        scratch = sb("scratch", [P, max(T * COLS // 2 + GPAD * T // 2, 7680)])

        def carve(at, a, b):
            return scratch[:, at:at + a * b].rearrange("p (a b) -> p a b", a=a)

        in_tile = scratch[:, 0:T * COLS // 2].bitcast(BF16).rearrange("p (t c) -> p t c", t=T)
        below = scratch[0:1, T * COLS // 2:T * COLS // 2 + GPAD * T // 2].bitcast(BF16).rearrange("p (g t) -> p g t", t=T)
        msg = carve(0, QUAD, HD)
        tmp = carve(2048, 2, HD)
        neg = carve(3072, 2, HD)
        pose = carve(4096, 2, HD)
        final = carve(5120, 2, C)
        ohT = carve(5632, 2, QUAD * P)
        featT = carve(6656, 2, HD)

        wh = carve(0, 4, C)
        wo = carve(4 * C, 2, HD)

        scratch2 = sb("scratch2", [P, 7 * COLS])

        def row_of(n, width=COLS):
            return scratch2[:, n * COLS:n * COLS + width]

        lo_i, tile_f, pos, pos_i = row_of(0).bitcast(I32), row_of(1), row_of(2), row_of(3).bitcast(I32)
        rank = row_of(4, 2 * COLS).rearrange("p (a c) -> p a c", a=2)
        w_b = row_of(6, COLS // 2).bitcast(BF16)
        s_odd = row_of(4, CHP)
        iota_i = row_of(2, 512).bitcast(I32)
        stage = row_of(0, 2 * W1).rearrange("p (a c) -> p a c", a=2)

        at = 2 * W1
        head_mean = scratch2[:, at:at + T * HEADS].rearrange("p (t h) -> p t h", h=HEADS)
        head_var = scratch2[:, at + T * HEADS:at + 2 * T * HEADS].rearrange("p (t h) -> p t h", h=HEADS)

        xs = sb("xs", [P, T, C])
        work = sb("work", [P, T, HD])
        stats = sb("stats", [P, T, 6])
        mv = sb("mv", [P, T, 2])
        rstd = sb("rstd", [P, T])
        nbias = sb("nbias", [P, T])
        norm = work[:, :, 0:C]
        acc_a = work[:, :, C:C + HALF]
        acc_b = work[:, :, C + HALF:HD]
        s_src1 = sb("s_src1", [P, T + 1, HEADS])
        s_src2 = sb("s_src2", [P, T + 1, 1])

        nat = {k: sb(f"nat_{k}", [P, COLS], I32) for k in ("src", "dst")}
        nat_w = sb("nat_w", [P, COLS])
        key_lo = sb("key_lo", [P, COLS])
        w_part = sb("w_part", [P, 3, COLS])
        index = sb("index", [P, 2, COLS])
        count = sb("count", [P, T])
        cap_i = sb("cap_i", [P, T], I32)
        cap = sb("cap", [P, T])
        cap_sum = sb("cap_sum", [P, T])
        first = sb("first", [P, T])
        chunk = sb("chunk", [P, COLS])
        lane = sb("lane", [P, COLS])
        tile_sum = sb("tile_sum", [1, GPAD])
        group_tile = {o: sb(f"group_tile_{o}", [1, GPAD], I32) for o in "SD"}

        oh_chunk = sb("oh_chunk", [P, RING, CHP], BF16)
        oh_w = sb("oh_w", [P, RING, 3, P], BF16)
        oh_i1 = sb("oh_i1", [P, RING, P], FP16)
        oh_i2 = sb("oh_i2", [P, RING, P], BF16)
        oh_lo = sb("oh_lo", [P, RING, P], BF16)
        s_lo = {o: sb(f"s_lo_{o}", [P, CHP]) for o in "SD"}
        s_idx = {o: sb(f"s_idx_{o}", [P, CHP], I32) for o in "SD"}
        s_w = {o: sb(f"s_w_{o}", [P, CHP]) for o in "SD"}
        rdeg = {o: sb(f"rdeg_{o}", [P, T]) for o in "SD"}

        idx_now = sb("idx_now", [P, 2, SLOTS], I32)
        rows = sb("rows", [P, SLOTS, W1])
        oh = sb("oh", [P, SLOTS, P])
        score = sb("score", [P, 2, QUAD * HEADS])
        lrelu = sb("lrelu", [P, 2, QUAD * HEADS])
        e_att = sb("e_att", [P, 2, QUAD * HEADS])

        whT = sb("whT", [P, 2, HD])
        ah = sb("ah", [P, 4 * 2 * HEADS])
        ahT = sb("ahT", [P, 2, 2 * HEADS])
        bh_col = sb("bh_col", [P, 4])
        bh_row = sb("bh_row", [1, HD])
        bah = sb("bah", [1, 2 * HEADS])
        gh = sb("gh", [P, HD])
        betah = sb("betah", [P, HD])
        woT = sb("woT", [P, 4, C])
        ao = sb("ao", [P, 4])
        aoT = sb("aoT", [P, 4, 2])
        bo_col = sb("bo_col", [P, 2])
        bo_row = sb("bo_row", [1, C])
        bao = sb("bao", [1, 2])
        go = sb("go", [P, C])
        betao = sb("betao", [P, C])

        q_pad = sem("q_pad")
        q_x = sem("q_x")
        q_edges = sem("q_edges")
        q_weights = sem("q_weights")
        iota_made = sem("iota_made")
        consts_made = sem("consts_made")
        dve_chain = sem("dve_chain")
        act_chain = sem("act_chain")
        pe_chain = sem("pe_chain")
        w_evac = sem("w_evac")
        counted = sem("counted")
        offsets = sem("offsets")
        col_ready = {o: sem(f"col_ready_{o}") for o in "SD"}
        col_free = {o: sem(f"col_free_{o}") for o in "SD"}
        sorted_psum = {o: sem(f"sorted_psum_{o}") for o in "SD"}
        edges_sorted = {o: sem(f"edges_sorted_{o}") for o in "SD"}
        var_ready = sem("var_ready")
        std_ready = sem("std_ready")
        nb_ready = sem("nb_ready")
        normed = sem("normed")
        tab_ab = sem("tab_ab")
        tab_1 = [sem(f"tab_1{i}") for i in range(2)]
        tab_2 = [sem(f"tab_2{i}") for i in range(2)]
        gathered = [sem(f"gathered{i}") for i in range(SLOTS)]
        idx_ready = sem("idx_ready")
        chunks_summed = sem("chunks_summed")
        oh_ready = {o: sem(f"oh_ready_{o}") for o in "SD12"}
        sum_ready = {o: sem(f"sum_ready_{o}") for o in "12"}
        sum_free = {o: sem(f"sum_free_{o}") for o in "SD12"}
        ohT_psum = {o: sem(f"ohT_psum_{o}") for o in "12"}
        ohT_ready = {o: sem(f"ohT_ready_{o}") for o in "12"}
        ssrc_ready = {o: sem(f"ssrc_ready_{o}") for o in "12"}
        z_ready = {o: sem(f"z_ready_{o}") for o in "12"}
        lrelu_ready = {o: sem(f"lrelu_ready_{o}") for o in "12"}
        e_ready = {o: sem(f"e_ready_{o}") for o in "12"}
        msg_ready = {o: sem(f"msg_ready_{o}") for o in "12"}
        l0_done = sem("l0_done")
        featT_psum = {o: sem(f"featT_psum_{o}") for o in "12"}
        featT_ready = {o: sem(f"featT_ready_{o}") for o in "12"}
        dense_psum = {o: sem(f"dense_psum_{o}") for o in "12"}
        dense_act = {o: sem(f"dense_act_{o}") for o in "12"}
        dense_dve = {o: sem(f"dense_dve_{o}") for o in "12"}
        elu_in = sem("elu_in")
        elu_out = sem("elu_out")
        z_done = sem("z_done")
        elu2_in = sem("elu2_in")
        elu2_out = sem("elu2_out")
        final_ready = sem("final_ready")
        q_out = [sem(f"q_out{i}") for i in range(2)]

        block = ctx.enter_context(nc.Block())
        WEIGHT_DMAS = 4 + 12

        @block.sync
        def _(sp):
            sp.wait_ge(q_pad, 4)
            for k, d in (("src", src), ("dst", dst)):
                sp.dma_start(nat[k][0:P - 1, :], d[0:(P - 1) * COLS].rearrange("(p c) -> p c", c=COLS)).then_inc(q_edges, 16)
                sp.dma_start(nat[k][P - 1:P, 0:TAIL], d[(P - 1) * COLS:E][None, :]).then_inc(q_edges, 16)
            sp.dma_start(nat_w[0:P - 1, :], edge_weight[0:(P - 1) * COLS].rearrange("(p c) -> p c", c=COLS)).then_inc(q_edges, 16)
            sp.dma_start(nat_w[P - 1:P, 0:TAIL], edge_weight[(P - 1) * COLS:E][None, :]).then_inc(q_edges, 16)
            sp.dma_start(xs[:, 0:T - 1, :], x[0:(T - 1) * P, :].rearrange("(t p) c -> p t c", p=P)).then_inc(q_x, 16)
            sp.dma_start(xs[0:LAST, T - 1, :], x[(T - 1) * P:N, :]).then_inc(q_x, 16)
            sp.dma_start(wh[:, :, :], W_heads.rearrange("(k q) d f -> (q d) k f", q=2)).then_inc(q_weights, 16)
            for q in range(2):
                for s in range(2):
                    sp.dma_start(ah[D * q:D * q + D, q + HEADS * s:q + HEADS * s + 18 * 3 + 1:18],
                                 a_heads.rearrange("(k q) (s d) -> q s d k", q=2, s=2)[q, s]).then_inc(q_weights, 16)
            sp.dma_start(bh_col[:, :], b_heads.rearrange("(k q) d -> (q d) k", q=2)).then_inc(q_weights, 16)
            sp.dma_start(bh_row[:, :], b_heads.rearrange("h d -> (h d)")[None, :]).then_inc(q_weights, 16)
            sp.dma_start(gh[:, :], g_heads.rearrange("h d -> (h d)").partition_broadcast(P)).then_inc(q_weights, 16)
            sp.dma_start(betah[:, :], beta_heads.rearrange("h d -> (h d)").partition_broadcast(P)).then_inc(q_weights, 16)
            sp.dma_start(wo[:, :, :], W_out.rearrange("(k p) f -> p k f", p=P)).then_inc(q_weights, 16)
            sp.dma_start(ao[:, :], a_out.rearrange("(a p) -> p a", p=P)).then_inc(q_weights, 16)
            sp.dma_start(bo_col[:, :], b_out.rearrange("(k p) -> p k", p=P)).then_inc(q_weights, 16)
            sp.dma_start(bo_row[:, :], b_out[None, :]).then_inc(q_weights, 16)
            sp.dma_start(go[:, :], g_out.partition_broadcast(P)).then_inc(q_weights, 16)
            sp.dma_start(betao[:, :], beta_out.partition_broadcast(P)).then_inc(q_weights, 16)

            sp.wait_ge(normed, T)
            for table, half in ((table_a, 0), (table_b, 1)):
                sp.dma_start(table.rearrange("(t p) c -> p t c", p=P),
                             work[:, :, half * HALF:(half + 1) * HALF]).then_inc(tab_ab, 16)

            for o, table, width, landed in (("1", table_1, W1, tab_1), ("2", table_2, W2, tab_2)):
                for t in range(T):
                    sp.wait_ge(dense_act[o], t + 1)
                    sp.wait_ge(dense_dve[o], t + 1)
                    sp.dma_start(table[t * P:(t + 1) * P, :], stage[:, t % 2, 0:width]).then_inc(landed[t % 2], 16)

            for t in range(T):
                n = P if t < T - 1 else LAST
                sp.wait_ge(final_ready, t + 1)
                sp.dma_start(out[t * P:t * P + n, :], final[0:n, t % 2, :]).then_inc(q_out[t % 2], 16)
            sp.wait_ge(q_out[0], 16 * ((T + 1) // 2))
            sp.wait_ge(q_out[1], 16 * (T // 2))

        @block.gpsimd
        def _(pool):
            nc.gpsimd.iota(iota_i[:, :], pattern=[[1, 512]], base=0, channel_multiplier=0).then_inc(iota_made, 1)
            nc.gpsimd.iota(row_i[:, :], pattern=[[0, 1]], base=0, channel_multiplier=1).then_inc(iota_made, 1)

            def round_indices(phase, order, r, u):
                nc.gpsimd.tensor_copy(idx_now[:, u, :], s_idx[order][:, bass.ds(r * SLOTS, SLOTS)]).then_inc(idx_ready, 1)
                pool.wait_ge(idx_ready, r + (phase * ROUNDS + 1))

            def gather(table, width, u, b):
                nc.gpsimd.indirect_dma_start(
                    out=rows[:, b, 0:width], out_offset=None, in_=table[:, :],
                    in_offset=bass.IndirectOffsetOnAxis(ap=idx_now[:, u, b:b + 1], axis=0),
                ).then_inc(gathered[b], 16)

            def gather_layer0(phase, order, table):
                with pool.Fori(0, ROUNDS // 2) as i:
                    for u in range(2):
                        round_indices(phase, order, i * 2 + u, u)
                        for b in range(SLOTS):
                            pool.wait_ge(chunks_summed, i * (2 * SLOTS) + (u * SLOTS + phase * CHUNKS + b + 1))
                            pool.nop(nofuse=True)
                            gather(table, HALF, u, b)

            def gather_layer1(o, table, width):
                phase = 1 + int(o)

                def later_round(r, u):
                    round_indices(phase, "S", r, u)
                    for b in range(SLOTS):
                        pool.wait_ge(msg_ready[o], r * SLOTS + (b + 1 - SLOTS))
                        pool.nop(nofuse=True)
                        gather(table, width, u, b)

                round_indices(phase, "S", 0, 0)
                for b in range(SLOTS):
                    gather(table, width, 0, b)
                later_round(1, 1)
                with pool.Fori(1, ROUNDS // 2) as i:
                    for u in range(2):
                        later_round(i * 2 + u, u)

            pool.wait_ge(edges_sorted["S"], 1)
            pool.wait_ge(tab_ab, 32)
            gather_layer0(0, "S", table_a)
            pool.wait_ge(edges_sorted["D"], 1)
            gather_layer0(1, "D", table_b)
            pool.wait_ge(tab_1[0], 16 * ((T + 1) // 2))
            pool.wait_ge(tab_1[1], 16 * (T // 2))
            gather_layer1("1", table_1, W1)
            pool.wait_ge(tab_2[0], 16 * ((T + 1) // 2))
            pool.wait_ge(tab_2[1], 16 * (T // 2))
            gather_layer1("2", table_2, W2)

        @block.scalar
        def _(act):
            def normalise(round_):
                act.wait_ge(var_ready, round_ + 1)
                nc.scalar.activation(rstd[:, :], mv[:, :, 1], ACT.Sqrt, bias=eps[:, :]).then_inc(std_ready, 1)
                act.wait_ge(nb_ready, round_ + 1)
                for t in range(T):
                    nc.scalar.activation(norm[:, t, :], xs[:, t, :], ACT.Relu, bias=nbias[:, t:t + 1],
                                         scale=rstd[:, t:t + 1]).then_inc(normed, 1)

            normalise(0)
            act.wait_ge(l0_done, 1)
            normalise(1)

            def dense(o, width, landed):
                for t in range(T + 1):
                    if t < T:
                        act.wait_ge(featT_psum[o], t + 1)
                        if t >= 2:
                            act.wait_ge(dense_psum[o], t - 1)
                        nk = width_in[o]
                        nc.scalar.copy(featT[:, t % 2, 0:nk], bank[t % 2][:, 0:nk]).then_inc(featT_ready[o], 1)
                    if t >= 1:
                        u = t - 1
                        act.wait_ge(dense_psum[o], u + 1)
                        if u >= 2:
                            act.wait_ge(landed[u % 2], 16 * (u // 2))
                        nc.scalar.copy(stage[:, u % 2, 0:width], bank[2 + u % 2][:, 0:width]).then_inc(dense_act[o], 1)

            def attend(o):
                heads = HEADS if o == "1" else 1

                def transposed(q, u):
                    act.wait_ge(ohT_psum[o], q + 1)
                    nc.scalar.copy(ohT[:, u, :], bank[u][:, :]).then_inc(ohT_ready[o], 1)

                def step(q, u):
                    act.wait_ge(lrelu_ready[o], q + 1)
                    nc.scalar.activation(e_att[:, u, 0:QUAD * heads], lrelu[:, u, 0:QUAD * heads], ACT.Exp,
                                         scale=-1.0).then_inc(e_ready[o], 1)
                    transposed(q + 1, 1 - u)

                transposed(0, 0)
                with act.Fori(0, QUADS // 2) as i:
                    for u in range(2):
                        step(i * 2 + u, u)

            width_in = {"1": C, "2": HD}
            dense("1", HD, tab_1)
            attend("1")
            act.wait_ge(var_ready, 3)
            nc.scalar.activation(head_var[:, :, :], head_var[:, :, :], ACT.Sqrt, bias=eps[:, :], scale=1.0 / D).then_inc(std_ready, 1)
            for t in range(T):
                act.wait_ge(elu_in, t + 1)
                nc.scalar.activation(neg[:, t % 2, :], neg[:, t % 2, :], ACT.Exp).then_inc(elu_out, 1)
            dense("2", C, tab_2)
            attend("2")
            act.wait_ge(var_ready, 4)
            nc.scalar.activation(rstd[:, :], mv[:, :, 1], ACT.Sqrt, bias=eps[:, :]).then_inc(std_ready, 1)
            for t in range(T):
                act.wait_ge(elu2_in, t + 1)
                nc.scalar.activation(neg[:, t % 2, 0:C], neg[:, t % 2, 0:C], ACT.Exp).then_inc(elu2_out, 1)

        @block.tensor
        def _(pe):
            pe.wait_ge(consts_made, 1)
            pe.wait_ge(q_weights, 16 * 15)
            for k in range(4):
                for m in range(2):
                    nc.tensor.transpose(bank[m][:, k * P:(k + 1) * P], wh[:, k, m * P:(m + 1) * P], ident[:, :])
            for k in range(2):
                for m in range(4):
                    b = bank[2 + m // 2][:, (m % 2) * C + k * P:(m % 2) * C + (k + 1) * P]
                    nc.tensor.transpose(b, wo[:, k, m * P:(m + 1) * P], ident[:, :])
            for m in range(2):
                for k in range(4):
                    nc.tensor.matmul(bank[4][:, m * 16:m * 16 + 16], wh[:, k, m * P:(m + 1) * P],
                                     ah[:, k * 16:(k + 1) * 16], start=(k == 0), stop=(k == 3))
            for m in range(4):
                for k in range(2):
                    nc.tensor.matmul(bank[4][:, 32 + 2 * m:34 + 2 * m], wo[:, k, m * P:(m + 1) * P],
                                     ao[:, k:k + 3:2], start=(k == 0), stop=(k == 1))
            for k in range(4):
                nc.tensor.matmul(bank[5][0:1, 0:16], bh_col[:, k:k + 1], ah[:, k * 16:(k + 1) * 16],
                                 start=(k == 0), stop=(k == 3))
            for k in range(2):
                last = nc.tensor.matmul(bank[5][0:1, 16:18], bo_col[:, k:k + 1], ao[:, k:k + 3:2],
                                        start=(k == 0), stop=(k == 1))
            last.then_inc(pe_chain, 1)

            def prefix(n):
                pe.wait_ge(counted, n + 1)
                nc.tensor.matmul(bank[6][:, 0:T], before[:, :], count[:, :], start=True, stop=True)
                nc.tensor.matmul(bank[7][:, 0:T], ones[:, 0:P], count[:, :], start=True, stop=True).then_inc(offsets, 1)

            def sort_open():
                for b in range(6):
                    nc.tensor.matmul(bank[b][:, :CHP if b < 5 else T], zero_lhs[:, :], oh_zero(b), start=True, stop=False)

            def oh_zero(b):
                return iota_chunk[:, 0:CHP if b < 5 else T]

            def sort_close(o):
                for b in range(6):
                    last = nc.tensor.matmul(bank[b][:, :CHP if b < 5 else T], zero_lhs[:, :], oh_zero(b), start=False, stop=True)
                last.then_inc(sorted_psum[o], 1)

            def sort_column(o, c, slot):
                pe.wait_ge(col_ready[o], c + 1)
                lhs = [oh_w[:, slot, f, :] for f in range(3)] + [oh_i1[:, slot, :], oh_i2[:, slot, :]]
                for b in range(5):
                    nc.tensor.matmul(bank[b][:, 0:CHP], lhs[b], oh_chunk[:, slot, :], start=False, stop=False)
                nc.tensor.matmul(bank[5][:, 0:T], oh_lo[:, slot, :], in_tile[:, :, bass.ds(c, 1)].rearrange("p t c -> p (t c)"),
                                 start=False, stop=False).then_inc(col_free[o], 1)

            def sum_rows(o, phase, i, k):
                c = i * SLOTS + k
                g = i * (SLOTS // GP) + k // GP
                if k % GP == 0:
                    pe.wait_ge(sum_free[o], g + 1)
                pe.wait_ge(oh_ready[o], c + 1)
                pe.wait_ge(gathered[k], i * 16 + 16 * (phase * ROUNDS + 1))
                nc.tensor.matmul(bank[6 + (k // GP) % 2][:, 0:HALF], oh[:, k, :], rows[:, k, 0:HALF],
                                 start=(k % GP == 0), stop=(k % GP == GP - 1)).then_inc(chunks_summed, 1)

            prefix(0)
            pe.wait_ge(w_evac, 1)
            sort_open()
            with pe.Fori(0, SORT_ROUNDS) as i:
                for k in range(SLOTS):
                    sort_column("S", i * SLOTS + k, k % RING)
            sort_close("S")
            prefix(1)
            pe.wait_ge(edges_sorted["S"], 1)
            sort_open()
            with pe.Fori(0, SORT_ROUNDS) as i:
                for k in range(SLOTS):
                    sort_column("D", i * SLOTS + k, k % RING)
                    sum_rows("S", 0, i, k)
            with pe.Fori(SORT_ROUNDS, ROUNDS) as i:
                for k in range(SLOTS):
                    sum_rows("S", 0, i, k)
            sort_close("D")
            with pe.Fori(0, ROUNDS) as i:
                for k in range(SLOTS):
                    sum_rows("D", 1, i, k)

            def dense(o, nk, width, rhs, rhs_s, b_row, b_s, ns, feats_ready, feat):
                for t in range(T + 1):
                    if t < T:
                        feats_ready(t)
                        if t >= 2:
                            pe.wait_ge(featT_ready[o], t - 1)
                        for k in range(nk):
                            last = nc.tensor.transpose(bank[t % 2][:, k * P:(k + 1) * P], feat[:, t, k * P:(k + 1) * P], ident[:, :])
                        last.then_inc(featT_psum[o], 1)
                    if t >= 1:
                        u = t - 1
                        pe.wait_ge(featT_ready[o], u + 1)
                        if u >= 2:
                            pe.wait_ge(dense_act[o], u - 1)
                            pe.wait_ge(dense_dve[o], u - 1)
                        nc.tensor.matmul(bank[2 + u % 2][:, 0:width], ones[0:1, 0:P], b_row[0:1, :], start=True, stop=False)
                        for k in range(nk):
                            nc.tensor.matmul(bank[2 + u % 2][:, 0:width], featT[:, u % 2, k * P:(k + 1) * P], rhs[:, k, :],
                                             start=False, stop=(k == nk - 1))
                        nc.tensor.matmul(bank[4 + u % 2][:, 0:ns], ones[0:1, 0:P], b_s[0:1, :], start=True, stop=False)
                        for k in range(nk):
                            last = nc.tensor.matmul(bank[4 + u % 2][:, 0:ns], featT[:, u % 2, k * P:(k + 1) * P], rhs_s[:, k, :],
                                                    start=False, stop=(k == nk - 1))
                        last.then_inc(dense_psum[o], 1)

            def attend(o):
                heads, width, s_src = (HEADS, HD, s_src1) if o == "1" else (1, C, s_src2)

                def transposed(q, u):
                    pe.wait_ge(oh_ready[o], q + 1)
                    for k in range(QUAD):
                        last = nc.tensor.transpose(bank[u][:, k * P:(k + 1) * P], oh[:, u * QUAD + k, :], ident[:, :])
                    last.then_inc(ohT_psum[o], 1)

                def source_scores(q, u):
                    tiles = [pe.value_load(group_tile["S"][0:1, bass.ds(q * 2 + j, 1)], min_val=0, max_val=T - 1) for j in range(2)]
                    pe.wait_ge(ohT_ready[o], q + 1)
                    for k in range(QUAD):
                        last = nc.tensor.matmul(bank[2 + u][:, k * heads:(k + 1) * heads], ohT[:, u, k * P:(k + 1) * P],
                                                s_src[:, bass.ds(tiles[k // 2], 1), :].rearrange("p t h -> p (t h)"),
                                                start=True, stop=True)
                    last.then_inc(ssrc_ready[o], 1)

                def step(q, u):
                    transposed(q + 1, 1 - u)
                    source_scores(q + 1, 1 - u)
                    for k in range(QUAD):
                        if k % 2 == 0:
                            pe.wait_ge(sum_free[o], q * 2 + (k // 2 + 1))
                        pe.wait_ge(msg_ready[o], q * QUAD + (k + 1))
                        mm = nc.tensor.matmul(bank[4 + 2 * u + k // 2][:, 0:width], oh[:, u * QUAD + k, :], msg[:, k, 0:width],
                                              start=(k % 2 == 0), stop=(k % 2 == 1))
                        if k % 2 == 1:
                            mm.then_inc(sum_ready[o], 1)

                transposed(0, 0)
                source_scores(0, 0)
                with pe.Fori(0, QUADS // 2) as i:
                    for u in range(2):
                        step(i * 2 + u, u)

            pe.wait_ge(edges_sorted["D"], 1)
            dense("1", 2, HD, whT, ahT, bh_row, bah, 2 * HEADS, lambda t: pe.wait_ge(normed, T + t + 1), norm)
            pe.wait_ge(dense_act["1"], T)
            pe.wait_ge(dense_dve["1"], T)
            attend("1")
            dense("2", 4, C, woT, aoT, bo_row, bao, 2, lambda t: pe.wait_ge(z_done, t + 1), work)
            pe.wait_ge(dense_act["2"], T)
            pe.wait_ge(dense_dve["2"], T)
            attend("2")

        @block.vector
        def _(dve):
            v = nc.vector
            linked = [0]

            def link(ins):
                linked[0] += 1
                ins.then_inc(dve_chain, 1)
                dve.wait_ge(dve_chain, linked[0])

            v.memset(nat["src"][:, :], T * P).then_inc(q_pad, 1)
            v.memset(nat["dst"][:, :], T * P).then_inc(q_pad, 1)
            v.memset(nat_w[:, :], 0.0).then_inc(q_pad, 1)
            v.memset(ah[:, :], 0.0)
            v.memset(xs[:, T - 1, :], 0.0).then_inc(q_pad, 1)
            v.memset(ones[:, :], 1.0)
            v.memset(zero_lhs[:, :], 0.0)
            v.memset(eps[:, :], EPS)
            v.memset(s_src1[:, T, :], 0.0)
            v.memset(s_src2[:, T, :], 0.0)
            dve.wait_ge(iota_made, 2)
            link(v.tensor_copy(iota_f[:, :], iota_i[:, :]))
            link(v.tensor_copy(row_f[:, :], row_i[:, :]))
            v.tensor_copy(iota_lane[:, :], iota_i[:, 0:P])
            v.tensor_copy(iota_chunk[:, :], iota_i[:, 0:CHP])
            v.tensor_scalar(ident[:, :], iota_f[:, 0:P], row_f[:, :], None, ALU.is_equal)
            link(v.tensor_scalar(before[:, :], iota_f[:, 0:P], row_f[:, :], None, ALU.is_gt))
            dve.sem_inc(consts_made, 1)
            dve.sem_inc(chunks_summed, SLOTS)
            for o in "SD":
                dve.sem_inc(col_free[o], RING)
                dve.sem_inc(sum_free[o], 2)

            def statistics():
                for t in range(T):
                    link(v.bn_stats(stats[:, t, :], xs[:, t, :]))
                    last = v.bn_aggr(mv[:, t, :], stats[:, t, :])
                last.then_inc(var_ready, 1)

            def scales(round_):
                dve.wait_ge(std_ready, round_ + 1)
                link(v.reciprocal(rstd[:, :], rstd[:, :]))
                v.scalar_tensor_tensor(out=nbias[:, :], in0=mv[:, :, 0], scalar=-1.0, in1=rstd[:, :],
                                       op0=ALU.mult, op1=ALU.mult).then_inc(nb_ready, 1)

            dve.wait_ge(q_x, 32)
            statistics()
            scales(0)

            dve.wait_ge(pe_chain, 1)
            for m in range(2):
                v.tensor_copy(whT[:, m, :], bank[m][:, :])
                v.tensor_copy(woT[:, 2 * m:2 * m + 2, :].rearrange("p k c -> p (k c)"), bank[2 + m][:, :])
            v.tensor_copy(ahT[:, :, :].rearrange("p k c -> p (k c)"), bank[4][:, 0:32])
            v.tensor_copy(aoT[:, :, :].rearrange("p k c -> p (k c)"), bank[4][:, 32:40])
            v.tensor_copy(bah[0:1, :], bank[5][0:1, 0:16])
            v.tensor_copy(bao[0:1, :], bank[5][0:1, 16:18]).then_inc(w_evac, 1)

            dve.wait_ge(q_edges, 96)
            link(v.tensor_copy(w_b[:, :], nat_w[:, :]))
            link(v.tensor_copy(w_part[:, 0, :], w_b[:, :]))
            link(v.tensor_sub(tile_f[:, :], nat_w[:, :], w_part[:, 0, :]))
            link(v.tensor_copy(w_b[:, :], tile_f[:, :]))
            link(v.tensor_copy(w_part[:, 1, :], w_b[:, :]))
            link(v.tensor_sub(w_part[:, 2, :], tile_f[:, :], w_part[:, 1, :]))

            def positions(o, n, key, other):
                link(v.tensor_scalar(lo_i[:, :], key[:, :], P - 1, None, ALU.bitwise_and))
                link(v.tensor_copy(key_lo[:, :], lo_i[:, :]))
                link(v.tensor_scalar(lo_i[:, :], key[:, :], 7, None, ALU.logical_shift_right))
                link(v.tensor_copy(tile_f[:, :], lo_i[:, :]))
                link(v.tensor_scalar(lo_i[:, :], other[:, :], 1, None, ALU.logical_shift_right))
                link(v.tensor_copy(index[:, 0, :], lo_i[:, :]))
                link(v.tensor_scalar(lo_i[:, :], other[:, :], 1, None, ALU.bitwise_and))
                link(v.tensor_copy(index[:, 1, :], lo_i[:, :]))
                link(v.scalar_tensor_tensor(out=index[:, 1, :], in0=index[:, 1, :], scalar=float(P), in1=key_lo[:, :],
                                            op0=ALU.mult, op1=ALU.add))
                link(v.tensor_scalar(index[:, 1, :], index[:, 1, :], 1.0, None, ALU.add))
                for t in range(T):
                    last = v.tensor_scalar(in_tile[:, t, :], tile_f[:, :], float(t), 0.0, ALU.is_equal, ALU.add,
                                           accum_out=count[:, t:t + 1])
                last.then_inc(counted, 1)
                dve.wait_ge(offsets, n + 1)
                link(v.tensor_scalar(cap[:, :], bank[7][:, 0:T], float(GP * P - 1), None, ALU.add))
                link(v.tensor_copy(cap_i[:, :], cap[:, :]))
                link(v.tensor_scalar(cap_i[:, :], cap_i[:, :], 8, None, ALU.logical_shift_right))
                link(v.tensor_copy(cap[:, :], cap_i[:, :]))
                link(v.tensor_tensor_scan(cap_sum[:, :], ones[:, 0:T], cap[:, :], 0.0, ALU.mult, ALU.add))
                link(v.tensor_sub(first[:, :], cap_sum[:, :], cap[:, :]))
                link(v.scalar_tensor_tensor(out=first[:, :], in0=first[:, :], scalar=float(GP * P), in1=bank[6][:, 0:T],
                                            op0=ALU.mult, op1=ALU.add))
                link(v.tensor_tensor(below[0:1, :, :], cap_sum[0:1, :].unsqueeze(1).to_broadcast([1, GPAD, T]),
                                     iota_f[0:1, 0:GPAD].unsqueeze(2).to_broadcast([1, GPAD, T]), ALU.is_le))
                link(v.tensor_reduce(tile_sum[0:1, :], below[0:1, :, :], AX.X, ALU.add))
                link(v.tensor_scalar(tile_sum[0:1, :], tile_sum[0:1, :], float(T - 1), None, ALU.min))
                link(v.tensor_copy(group_tile[o][0:1, :], tile_sum[0:1, :]))
                link(v.memset(pos[:, :], NO_POS))
                for t in range(T):
                    link(v.tensor_tensor_scan(rank[:, t % 2, :], ones[:, :], in_tile[:, t, :], first[:, t:t + 1], ALU.mult, ALU.add))
                    last = v.copy_predicated(pos[:, :], in_tile[:, t, :].bitcast(U16), rank[:, t % 2, :])
                link(last)
                link(v.tensor_scalar(pos[:, :], pos[:, :], -1.0, None, ALU.add))
                link(v.tensor_copy(pos_i[:, :], pos[:, :]))
                link(v.tensor_scalar(lo_i[:, :], pos_i[:, :], P - 1, None, ALU.bitwise_and))
                link(v.tensor_copy(lane[:, :], lo_i[:, :]))
                link(v.tensor_scalar(lo_i[:, :], pos_i[:, :], 7, None, ALU.logical_shift_right))
                link(v.tensor_copy(chunk[:, :], lo_i[:, :]))

            def sort_column(o, c, slot):
                dve.wait_ge(col_free[o], c + 1)
                at = lane[:, bass.ds(c, 1)]
                v.tensor_scalar(oh_chunk[:, slot, :], iota_chunk[:, :], chunk[:, bass.ds(c, 1)], None, ALU.is_equal)
                for f in range(3):
                    v.tensor_scalar(oh_w[:, slot, f, :], iota_lane[:, :], at, w_part[:, f, bass.ds(c, 1)], ALU.is_equal, ALU.mult)
                v.tensor_scalar(oh_i1[:, slot, :], iota_lane[:, :], at, index[:, 0, bass.ds(c, 1)], ALU.is_equal, ALU.mult)
                v.tensor_scalar(oh_i2[:, slot, :], iota_lane[:, :], at, index[:, 1, bass.ds(c, 1)], ALU.is_equal, ALU.mult)
                v.tensor_scalar(oh_lo[:, slot, :], iota_lane[:, :], key_lo[:, bass.ds(c, 1)], None, ALU.is_equal).then_inc(col_ready[o], 1)

            def sorted_edges(o):
                dve.wait_ge(sorted_psum[o], 1)
                link(v.tensor_scalar(s_lo[o][:, :], bank[4][:, 0:CHP], -1.0, None, ALU.add))
                link(v.tensor_scalar(s_odd[:, :], s_lo[o][:, :], float(P), None, ALU.is_ge))
                link(v.scalar_tensor_tensor(out=s_idx[o][:, :], in0=bank[3][:, 0:CHP], scalar=2.0, in1=s_odd[:, :],
                                            op0=ALU.mult, op1=ALU.add))
                v.scalar_tensor_tensor(out=s_lo[o][:, :], in0=s_odd[:, :], scalar=-float(P), in1=s_lo[o][:, :],
                                       op0=ALU.mult, op1=ALU.add)
                link(v.tensor_copy(s_w[o][:, :], bank[0][:, 0:CHP]))
                link(v.tensor_add(s_w[o][:, :], s_w[o][:, :], bank[1][:, 0:CHP]))
                link(v.tensor_add(s_w[o][:, :], s_w[o][:, :], bank[2][:, 0:CHP]))
                link(v.tensor_scalar(rdeg[o][:, :], bank[5][:, 0:T], 1.0, None, ALU.max))
                link(v.reciprocal(rdeg[o][:, :], rdeg[o][:, :]))
                dve.sem_inc(edges_sorted[o], 1)

            def weighted_one_hot(o, phase, i, k):
                c = i * SLOTS + k
                dve.wait_ge(chunks_summed, c + (phase * CHUNKS + 1))
                v.tensor_scalar(oh[:, k, :], iota_f[:, 0:P], s_lo[o][:, bass.ds(c, 1)], s_w[o][:, bass.ds(c, 1)],
                                ALU.is_equal, ALU.mult).then_inc(oh_ready[o], 1)

            def add_group(o, acc, tile, g, psum, banks):
                dve.wait_ge(sum_free[o], g + banks)
                a = acc[:, bass.ds(tile, 1), :].rearrange("p t c -> p (t c)")
                v.tensor_add(a, a, psum).then_inc(sum_free[o], 1)

            def group_tiles(o, g, n):
                return [dve.value_load(group_tile[o][0:1, bass.ds(g + j, 1)], min_val=0, max_val=T - 1) for j in range(n)]

            def layer0_part(o, phase, acc, i, k, tiles):
                weighted_one_hot(o, phase, i, k)
                if k % GP == GP - 1:
                    dve.wait_ge(chunks_summed, i * SLOTS + (SLOTS + phase * CHUNKS + k + 1))
                    add_group(o, acc, tiles[k // GP], i * (SLOTS // GP) + k // GP, bank[6 + (k // GP) % 2][:, 0:HALF], 2)

            positions("S", 0, nat["src"], nat["dst"])
            with dve.Fori(0, SORT_ROUNDS) as i:
                for k in range(SLOTS):
                    sort_column("S", i * SLOTS + k, k % RING)
            sorted_edges("S")

            dve.wait_ge(tab_ab, 32)
            link(v.memset(work[:, :, C:HD], 0.0))
            positions("D", 1, nat["dst"], nat["src"])
            with dve.Fori(0, SORT_ROUNDS) as i:
                tiles = group_tiles("S", i * (SLOTS // GP), SLOTS // GP)
                for k in range(SLOTS):
                    sort_column("D", i * SLOTS + k, k % RING)
                    layer0_part("S", 0, acc_a, i, k, tiles)
            with dve.Fori(SORT_ROUNDS, ROUNDS) as i:
                tiles = group_tiles("S", i * (SLOTS // GP), SLOTS // GP)
                for k in range(SLOTS):
                    layer0_part("S", 0, acc_a, i, k, tiles)
            sorted_edges("D")
            with dve.Fori(0, ROUNDS) as i:
                tiles = group_tiles("D", i * (SLOTS // GP), SLOTS // GP)
                for k in range(SLOTS):
                    layer0_part("D", 1, acc_b, i, k, tiles)
            dve.wait_ge(sum_free["S"], GROUPS + 2)
            dve.wait_ge(sum_free["D"], GROUPS + 2)
            for o, acc, half in (("S", acc_a, xs[:, :, 0:HALF]), ("D", acc_b, xs[:, :, HALF:C])):
                link(v.tensor_tensor(acc, acc, rdeg[o][:, :].unsqueeze(2).to_broadcast([P, T, HALF]), ALU.mult))
                link(v.tensor_tensor(half, half, acc, ALU.add))
            dve.sem_inc(l0_done, 1)
            statistics()
            scales(1)

            def dense(o, width, ns, s_src, landed):
                for t in range(T):
                    dve.wait_ge(dense_psum[o], t + 1)
                    if t >= 2:
                        dve.wait_ge(landed[t % 2], 16 * (t // 2))
                    v.tensor_copy(s_src[:, t, :], bank[4 + t % 2][:, 0:ns])
                    v.tensor_copy(stage[:, t % 2, width:width + ns], bank[4 + t % 2][:, ns:2 * ns]).then_inc(dense_dve[o], 1)

            def attend(o):
                heads, width = (HEADS, HD) if o == "1" else (1, C)
                acc = work[:, :, 0:width]
                dve.sem_inc(sum_free[o], 4)

                def one_hots(q, u):
                    for k in range(QUAD):
                        last = v.tensor_scalar(oh[:, u * QUAD + k, :], iota_f[:, 0:P], s_lo["S"][:, bass.ds(q * QUAD + k, 1)],
                                               None, ALU.is_equal)
                    last.then_inc(oh_ready[o], 1)

                def scores(i, q, u):
                    dve.wait_ge(ssrc_ready[o], q + 1)
                    for k in range(QUAD):
                        dve.wait_ge(gathered[u * QUAD + k], i * 16 + 16 * ((1 + int(o)) * ROUNDS + 1))
                    n = QUAD * heads
                    v.tensor_tensor(score[:, u, 0:n].rearrange("p (k h) -> p k h", h=heads),
                                    bank[2 + u][:, 0:n].rearrange("p (k h) -> p k h", h=heads),
                                    rows[:, u * QUAD:(u + 1) * QUAD, width:width + heads], ALU.add).then_inc(z_ready[o], 1)
                    dve.wait_ge(z_ready[o], q + 1)
                    v.scalar_tensor_tensor(out=lrelu[:, u, 0:n], in0=score[:, u, 0:n], scalar=ALPHA, in1=score[:, u, 0:n],
                                           op0=ALU.mult, op1=ALU.max).then_inc(lrelu_ready[o], 1)

                def messages(q, u):
                    dve.wait_ge(e_ready[o], q + 1)
                    for k in range(QUAD):
                        row, e = rows[:, u * QUAD + k, 0:width], e_att[:, u, k * heads:(k + 1) * heads]
                        if heads == 1:
                            m = v.tensor_scalar(msg[:, k, 0:width], row, e, None, ALU.mult)
                        else:
                            m = v.tensor_tensor(msg[:, k, :].rearrange("p (h d) -> p h d", h=heads),
                                                row.rearrange("p (h d) -> p h d", h=heads),
                                                e.unsqueeze(2).to_broadcast([P, heads, D]), ALU.mult)
                        m.then_inc(msg_ready[o], 1)

                def add_groups(q, u, tiles):
                    for j in range(2):
                        dve.wait_ge(sum_ready[o], q * 2 + (j + 1))
                        add_group(o, acc, tiles[j], q * 2 + j, bank[4 + 2 * u + j][:, 0:width], 4)

                def step(i, q, u, tiles):
                    scores(i, q, u)
                    if tiles is not None:
                        add_groups(q - 1, 1 - u, tiles)
                    one_hots(q + 1, 1 - u)
                    messages(q, u)

                one_hots(0, 0)
                step(0, 0, 0, None)
                step(0, 1, 1, group_tiles("S", 0, 2))
                with dve.Fori(1, QUADS // 2) as i:
                    for u in range(2):
                        step(i, i * 2 + u, u, group_tiles("S", i * 4 + (2 * u - 2), 2))
                add_groups(QUADS - 1, 1, group_tiles("S", GROUPS - 2, 2))

            dense("1", HD, HEADS, s_src1, tab_1)
            link(v.memset(work[:, :, :], 0.0))
            attend("1")
            dve.wait_ge(sum_free["1"], GROUPS + 4)

            def per_head(a):
                return a.rearrange("p (h d) -> p h d", h=HEADS)

            for t in range(T):
                last = v.tensor_reduce(head_mean[:, t, :], per_head(work[:, t, :]), AX.X, ALU.add)
            link(last)
            link(v.tensor_scalar(head_mean[:, :, :], head_mean[:, :, :], 1.0 / D, None, ALU.mult))
            for t in range(T):
                y = per_head(work[:, t, :])
                link(v.tensor_tensor(y, y, head_mean[:, t, :].unsqueeze(2).to_broadcast([P, HEADS, D]), ALU.subtract))
                link(v.tensor_tensor(tmp[:, t % 2, :], work[:, t, :], work[:, t, :], ALU.mult))
                last = v.tensor_reduce(head_var[:, t, :], per_head(tmp[:, t % 2, :]), AX.X, ALU.add)
            last.then_inc(var_ready, 1)
            dve.wait_ge(std_ready, 3)
            link(v.reciprocal(head_var[:, :, :], head_var[:, :, :]))
            for t in range(T):
                y = per_head(work[:, t, :])
                link(v.tensor_tensor(y, y, head_var[:, t, :].unsqueeze(2).to_broadcast([P, HEADS, D]), ALU.mult))
                link(v.tensor_tensor(work[:, t, :], work[:, t, :], gh[:, :], ALU.mult))
                link(v.tensor_tensor(work[:, t, :], work[:, t, :], betah[:, :], ALU.add))
                v.tensor_scalar(neg[:, t % 2, :], work[:, t, :], 0.0, None, ALU.min).then_inc(elu_in, 1)
                link(v.tensor_scalar(pose[:, t % 2, :], work[:, t, :], 0.0, None, ALU.max))
                dve.wait_ge(elu_out, t + 1)
                v.scalar_tensor_tensor(out=work[:, t, :], in0=neg[:, t % 2, :], scalar=-1.0, in1=pose[:, t % 2, :],
                                       op0=ALU.add, op1=ALU.add).then_inc(z_done, 1)

            dense("2", C, 1, s_src2, tab_2)
            link(v.memset(work[:, :, 0:C], 0.0))
            attend("2")
            dve.wait_ge(sum_free["2"], GROUPS + 4)

            for t in range(T):
                link(v.bn_stats(stats[:, t, :], work[:, t, 0:C]))
                last = v.bn_aggr(mv[:, t, :], stats[:, t, :])
            last.then_inc(var_ready, 1)
            dve.wait_ge(std_ready, 4)
            link(v.reciprocal(rstd[:, :], rstd[:, :]))
            for t in range(T):
                y = work[:, t, 0:C]
                link(v.tensor_scalar(y, y, mv[:, t, 0:1], rstd[:, t:t + 1], ALU.subtract, ALU.mult))
                link(v.tensor_tensor(y, y, go[:, :], ALU.mult))
                link(v.tensor_tensor(y, y, betao[:, :], ALU.add))
                v.tensor_scalar(neg[:, t % 2, 0:C], y, 0.0, None, ALU.min).then_inc(elu2_in, 1)
                link(v.tensor_scalar(pose[:, t % 2, 0:C], y, 0.0, None, ALU.max))
                link(v.tensor_tensor(pose[:, t % 2, 0:C], pose[:, t % 2, 0:C], xs[:, t, :], ALU.add))
                dve.wait_ge(elu2_out, t + 1)
                if t >= 2:
                    dve.wait_ge(q_out[t % 2], 16 * (t // 2))
                v.scalar_tensor_tensor(out=final[:, t % 2, :], in0=neg[:, t % 2, 0:C], scalar=-1.0, in1=pose[:, t % 2, 0:C],
                                       op0=ALU.add, op1=ALU.add).then_inc(final_ready, 1)


_INS = ["x", "src", "dst", "edge_weight", "L1_gnn_W_heads", "L1_gnn_b_heads", "L1_gnn_a_heads", "L1_gnn_g_heads",
        "L1_gnn_beta_heads", "L1_gnn_W_out", "L1_gnn_b_out", "L1_gnn_a_out", "L1_gnn_g_out", "L1_gnn_beta_out"]


def kernel(**inputs):
    import numpy as _np
    import concourse.bacc as _bacc
    from concourse import mybir as _mybir
    from concourse.bass_utils import run_bass_kernel_spmd as _run

    nc = _bacc.Bacc("TRN2", target_bir_lowering=False, num_devices=1)
    arrays, args = {}, []
    for name in _INS:
        a = _np.ascontiguousarray(inputs[name])
        arrays[f"in_{name}"] = a
        args.append(nc.dram_tensor(f"in_{name}", a.shape, _mybir.dt.from_np(a.dtype), kind="ExternalInput").ap())
    args.append(nc.dram_tensor("out_x", (N, C), _mybir.dt.float32, kind="ExternalOutput").ap())
    build(nc, *args)
    return _run(nc, [arrays], core_ids=[0]).results[0]["out_x"]
```

```python
import concourse.bass as bass
from concourse import mybir
from contextlib import ExitStack

F32 = mybir.dt.float32
I32 = mybir.dt.int32
BF16 = mybir.dt.bfloat16
FP16 = mybir.dt.float16
U16 = mybir.dt.uint16
ALU = mybir.AluOpType
ACT = mybir.ActivationFunctionType
AX = mybir.AxisListType

P = 128
N = 3125
C = 256
HALF = C // 2
E = 53125
HEADS, D = 8, 64
HD = HEADS * D
T = -(-N // P)
LAST = N - (T - 1) * P
COLS = -(-E // P)
TAIL = E - (P - 1) * COLS
GP = 2
GROUPS = (E + T * (GP * P - 1)) // (GP * P)
CHUNKS = GROUPS * GP
QUAD = 4
QUADS = CHUNKS // QUAD
UNROLL = 4
SLOTS = UNROLL * QUAD
TILE_AT = 2
ROUNDS = CHUNKS // SLOTS
SORT_ROUNDS = COLS // SLOTS
RING = 4
W1 = HD + HEADS
W2 = C + 1
PAD_CHUNKS = -(-COLS // P)
PITCH = CHUNKS + PAD_CHUNKS
REC = 4
EPS = 1e-5
ALPHA = 0.2
assert CHUNKS % SLOTS == 0 and COLS % SLOTS == 0 and CHUNKS <= 512 and ROUNDS % 2 == 1 and RING * 4 == SLOTS


def build(nc, x, src, dst, edge_weight, W_heads, b_heads, a_heads, g_heads, beta_heads,
          W_out, b_out, a_out, g_out, beta_out, out):
    ctx = ExitStack()
    with ctx:
        def sb(name, shape, dt=F32):
            return ctx.enter_context(nc.sbuf_tensor(name, shape, dt))

        def sem(name):
            return ctx.enter_context(nc.semaphore(name))

        ctx.enter_context(nc.allow_non_contiguous_dma(reason="small weight vectors"))
        bank = [ctx.enter_context(nc.psum_tensor(f"bank{i}", [P, 512], F32)) for i in range(8)]

        table_a = nc.dram_tensor("table_a", (T * P, HALF), F32, kind="Internal").ap()
        table_b = nc.dram_tensor("table_b", (T * P, HALF), F32, kind="Internal").ap()
        records = nc.dram_tensor("records", (P * PITCH, REC), F32, kind="Internal").ap()
        table_1 = nc.dram_tensor("table_1", (T * P, W1), F32, kind="Internal").ap()
        table_2 = nc.dram_tensor("table_2", (T * P, W2), F32, kind="Internal").ap()

        iota_f = sb("iota_f", [P, 512])
        iota_lane = sb("iota_lane", [P, P], BF16)
        iota_chunk = sb("iota_chunk", [P, CHUNKS], FP16)
        row_i = sb("row_i", [P, 1], I32)
        row_f = sb("row_f", [P, 1])
        ident = sb("ident", [P, P])
        before = sb("before", [P, P])
        ones = sb("ones", [P, COLS])
        one_b = sb("one_b", [P, 1], BF16)
        eps = sb("eps", [P, 1])

        scratch = sb("scratch", [P, (COLS + GROUPS) * T // 2])

        def carve(at, a, b):
            return scratch[:, at:at + a * b].rearrange("p (a b) -> p a b", a=a)

        in_tile = scratch[:, 0:T * COLS // 2].bitcast(BF16).rearrange("p (t c) -> p t c", t=T)
        below = scratch[0:1, T * COLS // 2:(COLS + GROUPS) * T // 2].bitcast(BF16).rearrange("p (g t) -> p g t", t=T)
        msg = carve(0, 2 * QUAD, HD)
        tmp = carve(0, 2, HD)
        neg = carve(2 * HD, 2, HD)
        pose = carve(4 * HD, 2, HD)
        final = carve(6 * HD, 2, C)
        oh_count = scratch[:, 0:SLOTS * P // 2].bitcast(BF16).rearrange("p (a c) -> p a c", c=P)
        ohT = carve(8 * HD, 2, QUAD * P)
        featT = carve(10 * HD, 2, HD)
        scratch2 = sb("scratch2", [P, 7 * COLS])

        def row_of(n, width=COLS):
            return scratch2[:, n * COLS:n * COLS + width]

        lo_i, tile_f, pos, pos_i = row_of(0).bitcast(I32), row_of(1), row_of(2), row_of(3).bitcast(I32)
        rank = row_of(4, 2 * COLS).rearrange("p (a c) -> p a c", a=2)
        w_b = row_of(6, COLS // 2).bitcast(BF16)
        s_odd = row_of(4, CHUNKS)
        iota_i = row_of(2, 512).bitcast(I32)
        stage = row_of(0, 2 * W1).rearrange("p (a c) -> p a c", a=2)

        at = 2 * W1
        head_mean = scratch2[:, at:at + T * HEADS].rearrange("p (t h) -> p t h", h=HEADS)
        head_var = scratch2[:, at + T * HEADS:at + 2 * T * HEADS].rearrange("p (t h) -> p t h", h=HEADS)

        xs = sb("xs", [P, T, C])
        work = sb("work", [P, T, HD])
        stats = sb("stats", [P, T, 6])
        mv = sb("mv", [P, T, 2])
        rstd = sb("rstd", [P, T])
        nbias = sb("nbias", [P, T])
        norm = work[:, :, 0:C]
        acc = {"S": work[:, :, C:C + HALF + 1], "D": work[:, :, 0:HALF + 1]}
        s_src1 = sb("s_src1", [P, T, HEADS])
        s_src2 = sb("s_src2", [P, T, 1])

        given = sb("given", [P, 11, COLS])
        nat = {"src": given[:, 0, :].bitcast(I32), "dst": given[:, 1, :].bitcast(I32)}
        nat_w = given[:, 2, :]
        key_lo = given[:, 3, :]
        w_part = given[:, 4:7, :]
        index = given[:, 7:9, :]
        count = sb("count", [P, T])
        cap_i = sb("cap_i", [P, T], I32)
        cap = sb("cap", [P, T])
        cap_sum = sb("cap_sum", [P, T])
        first = sb("first", [P, T])
        chunk = given[:, 9, :]
        lane = given[:, 10, :]
        tile_sum = sb("tile_sum", [1, GROUPS])
        group_tile = {o: sb(f"group_tile_{o}", [1, TILE_AT + GROUPS], I32) for o in "SD"}

        sort_ring = sb("sort_ring", [P, RING, CHUNKS + 6 * P], BF16)
        oh_chunk = sort_ring[:, :, 0:CHUNKS]
        oh_w = sort_ring[:, :, CHUNKS:CHUNKS + 3 * P].rearrange("p r (f c) -> p r f c", c=P)
        oh_i1 = sort_ring[:, :, CHUNKS + 3 * P:CHUNKS + 4 * P].bitcast(FP16)
        oh_i2 = sort_ring[:, :, CHUNKS + 4 * P:CHUNKS + 5 * P]
        oh_lane = sort_ring[:, :, CHUNKS + 5 * P:CHUNKS + 6 * P]
        by_dst = sb("by_dst", [P, CHUNKS, REC])
        s_lo = {"S": sb("s_lo_S", [P, CHUNKS]), "D": by_dst[:, :, 2]}
        s_idx = {"S": sb("s_idx_S", [P, CHUNKS], I32), "D": by_dst[:, :, 1].bitcast(I32)}
        s_w = {"S": sb("s_w_S", [P, CHUNKS]), "D": by_dst[:, :, 0]}
        rdeg = sb("rdeg", [P, T, 1])

        idx_now = sb("idx_now", [P, 2, SLOTS], I32)
        rec_now = sb("rec_now", [P, 2, SLOTS, REC])
        rows_near = sb("rows_near", [P, SLOTS // 2, W1])
        rows_far = given[:, :, :].rearrange("p a c -> p (a c)")[:, 0:SLOTS // 2 * W1].rearrange("p (a c) -> p a c", c=W1)
        held = rows_near[:, :, :].rearrange("p a c -> p (a c)")
        rec = held[:, 0:REC * COLS].rearrange("p (c f) -> p c f", f=REC)
        rec_row = held[:, REC * COLS:(REC + 1) * COLS].bitcast(I32)
        rows0 = rows_near[:, :, :].rearrange("p a c -> p (a c)")[:, 0:SLOTS * HALF].rearrange("p (a c) -> p a c", c=HALF)

        def row_slots(a, n):
            return (rows_near if a < SLOTS // 2 else rows_far)[:, a % (SLOTS // 2):a % (SLOTS // 2) + n, :]

        oh = sb("oh", [P, SLOTS, P])
        oh_flat = oh[:, :, :].rearrange("p a c -> p (a c)")
        wh = oh_flat[:, 0:4 * C].rearrange("p (k c) -> p k c", c=C)
        wo = oh_flat[:, 4 * C:4 * C + 2 * HD].rearrange("p (k c) -> p k c", c=HD)
        score = sb("score", [P, 2, QUAD * HEADS])
        lrelu = sb("lrelu", [P, 2, QUAD * HEADS])
        e_att = sb("e_att", [P, 2, QUAD * HEADS])

        gains = sort_ring[:, :, :].rearrange("p r c -> p (r c)")[:, 0:4 * (HD + C)].bitcast(F32)
        gh, betah = gains[:, 0:HD], gains[:, HD:2 * HD]
        go, betao = gains[:, 2 * HD:2 * HD + C], gains[:, 2 * HD + C:2 * (HD + C)]
        whT = sb("whT", [P, 2, HD])
        ah = sb("ah", [P, 4 * 2 * HEADS])
        ahT = sb("ahT", [P, 2, 2 * HEADS])
        bh_col = sb("bh_col", [P, 4])
        bh_row = sb("bh_row", [1, HD])
        bah = sb("bah", [1, 2 * HEADS])
        woT = sb("woT", [P, 4, C])
        ao = sb("ao", [P, 4])
        aoT = sb("aoT", [P, 4, 2])
        bo_col = sb("bo_col", [P, 2])
        bo_row = sb("bo_row", [1, C])
        bao = sb("bao", [1, 2])

        q_pad = sem("q_pad")
        q_x = sem("q_x")
        q_edges = sem("q_edges")
        q_weights = sem("q_weights")
        q_gains = sem("q_gains")
        iota_made = sem("iota_made")
        consts_made = sem("consts_made")
        dve_chain = sem("dve_chain")
        act_chain = sem("act_chain")
        pe_chain = sem("pe_chain")
        w_evac = sem("w_evac")
        counted = sem("counted")
        offsets = sem("offsets")
        q_zero = sem("q_zero")
        acc_zeroed = sem("acc_zeroed")
        rec_ready = sem("rec_ready")
        rec_staged = sem("rec_staged")
        scattered = [sem(f"scattered{i}") for i in range(2)]
        q_by_dst = sem("q_by_dst")
        lane_ready = sem("lane_ready")
        fields_ready = sem("fields_ready")
        col_ready = sem("col_ready")
        col_free = sem("col_free")
        edges_sorted = sem("edges_sorted")
        stats_ready = sem("stats_ready")
        moments_ready = sem("moments_ready")
        var_ready = sem("var_ready")
        std_ready = sem("std_ready")
        nb_ready = sem("nb_ready")
        normed = sem("normed")
        tab_ab = sem("tab_ab")
        tab_1 = [sem(f"tab_1{i}") for i in range(2)]
        tab_2 = [sem(f"tab_2{i}") for i in range(2)]
        gathered = [sem(f"gathered{i}") for i in range(SLOTS)]
        idx_ready = sem("idx_ready")
        chunks_summed = sem("chunks_summed")
        oh_ready = {o: sem(f"oh_ready_{o}") for o in "SD12"}
        sum_ready = {o: sem(f"sum_ready_{o}") for o in "12"}
        sum_free = {o: sem(f"sum_free_{o}") for o in "SD12"}
        ohT_psum = {o: sem(f"ohT_psum_{o}") for o in "12"}
        ohT_ready = {o: sem(f"ohT_ready_{o}") for o in "12"}
        ssrc_ready = {o: sem(f"ssrc_ready_{o}") for o in "12"}
        z_ready = {o: sem(f"z_ready_{o}") for o in "12"}
        lrelu_ready = {o: sem(f"lrelu_ready_{o}") for o in "12"}
        e_ready = {o: sem(f"e_ready_{o}") for o in "12"}
        msg_ready = {o: sem(f"msg_ready_{o}") for o in "12"}
        l0_done = sem("l0_done")
        featT_psum = {o: sem(f"featT_psum_{o}") for o in "12"}
        featT_ready = {o: sem(f"featT_ready_{o}") for o in "12"}
        dense_psum = {o: sem(f"dense_psum_{o}") for o in "12"}
        dense_act = {o: sem(f"dense_act_{o}") for o in "12"}
        dense_dve = {o: sem(f"dense_dve_{o}") for o in "12"}
        elu_in = sem("elu_in")
        elu_out = sem("elu_out")
        z_done = sem("z_done")
        elu2_in = sem("elu2_in")
        elu2_out = sem("elu2_out")
        final_ready = sem("final_ready")
        q_out = [sem(f"q_out{i}") for i in range(2)]

        def tile_numbers(engine, o, at, n):
            return nc.values_load_multi_w_load_instructions(
                group_tile[o][0:1, bass.ds(at, n)], engines=[engine], min_val=0, max_val=T - 1,
                skip_runtime_bounds_check_because="clamped to T - 1 when made")[1]

        block = ctx.enter_context(nc.Block())
        WEIGHT_DMAS = 4 + 12

        @block.sync
        def _(sp):
            sp.wait_ge(q_pad, 4)
            sp.wait_ge(acc_zeroed, 1)
            zeros = work[:, 0:8, C:C + PITCH * REC // 8]
            sp.dma_start(records.rearrange("(p c) f -> p (c f)", p=P).rearrange("p (a b) -> p a b", a=8), zeros).then_inc(q_zero, 16)
            for k, d in (("src", src), ("dst", dst)):
                sp.dma_start(nat[k][0:P - 1, :], d[0:(P - 1) * COLS].rearrange("(p c) -> p c", c=COLS)).then_inc(q_edges, 16)
                sp.dma_start(nat[k][P - 1:P, 0:TAIL], d[(P - 1) * COLS:E][None, :]).then_inc(q_edges, 16)
            sp.dma_start(nat_w[0:P - 1, :], edge_weight[0:(P - 1) * COLS].rearrange("(p c) -> p c", c=COLS)).then_inc(q_edges, 16)
            sp.dma_start(nat_w[P - 1:P, 0:TAIL], edge_weight[(P - 1) * COLS:E][None, :]).then_inc(q_edges, 16)
            sp.dma_start(xs[:, 0:T - 1, :], x[0:(T - 1) * P, :].rearrange("(t p) c -> p t c", p=P)).then_inc(q_x, 16)
            sp.dma_start(xs[0:LAST, T - 1, :], x[(T - 1) * P:N, :]).then_inc(q_x, 16)
            sp.dma_start(wh[:, :, :], W_heads.rearrange("(k q) d f -> (q d) k f", q=2)).then_inc(q_weights, 16)
            for q in range(2):
                for s in range(2):
                    sp.dma_start(ah[D * q:D * q + D, q + HEADS * s:q + HEADS * s + 18 * 3 + 1:18],
                                 a_heads.rearrange("(k q) (s d) -> q s d k", q=2, s=2)[q, s]).then_inc(q_weights, 16)
            sp.dma_start(bh_col[:, :], b_heads.rearrange("(k q) d -> (q d) k", q=2)).then_inc(q_weights, 16)
            sp.dma_start(bh_row[:, :], b_heads.rearrange("h d -> (h d)")[None, :]).then_inc(q_weights, 16)
            sp.dma_start(wo[:, :, :], W_out.rearrange("(k p) f -> p k f", p=P)).then_inc(q_weights, 16)
            sp.dma_start(ao[:, :], a_out.rearrange("(a p) -> p a", p=P)).then_inc(q_weights, 16)
            sp.dma_start(bo_col[:, :], b_out.rearrange("(k p) -> p k", p=P)).then_inc(q_weights, 16)
            sp.dma_start(bo_row[:, :], b_out[None, :]).then_inc(q_weights, 16)

            sp.wait_ge(normed, T)
            for table, half in ((table_a, 0), (table_b, 1)):
                sp.dma_start(table.rearrange("(t p) c -> p t c", p=P),
                             work[:, :, half * HALF:(half + 1) * HALF]).then_inc(tab_ab, 16)

            for u in range(2):
                sp.wait_ge(scattered[u], 16 * SLOTS * (SORT_ROUNDS // 2))
            sp.dma_start(by_dst[:, :, :], records.rearrange("(p c) f -> p c f", p=P)[:, 0:CHUNKS, :]).then_inc(q_by_dst, 16)

            sp.wait_ge(l0_done, 1)
            sp.dma_start(gh[:, :], g_heads.rearrange("h d -> (h d)").partition_broadcast(P)).then_inc(q_gains, 16)
            sp.dma_start(betah[:, :], beta_heads.rearrange("h d -> (h d)").partition_broadcast(P)).then_inc(q_gains, 16)
            sp.dma_start(go[:, :], g_out.partition_broadcast(P)).then_inc(q_gains, 16)
            sp.dma_start(betao[:, :], beta_out.partition_broadcast(P)).then_inc(q_gains, 16)

            for o, table, width, landed in (("1", table_1, W1, tab_1), ("2", table_2, W2, tab_2)):
                for t in range(T):
                    sp.wait_ge(dense_act[o], t + 1)
                    sp.wait_ge(dense_dve[o], t + 1)
                    sp.dma_start(table[t * P:(t + 1) * P, :], stage[:, t % 2, 0:width]).then_inc(landed[t % 2], 16)

            for t in range(T):
                n = P if t < T - 1 else LAST
                sp.wait_ge(final_ready, t + 1)
                sp.dma_start(out[t * P:t * P + n, :], final[0:n, t % 2, :]).then_inc(q_out[t % 2], 16)
            sp.wait_ge(q_out[0], 16 * ((T + 1) // 2))
            sp.wait_ge(q_out[1], 16 * (T // 2))

        @block.gpsimd
        def _(pool):
            nc.gpsimd.iota(iota_i[:, :], pattern=[[1, 512]], base=0, channel_multiplier=0).then_inc(iota_made, 1)
            nc.gpsimd.iota(row_i[:, :], pattern=[[0, 1]], base=0, channel_multiplier=1).then_inc(iota_made, 1)

            def round_indices(phase, order, r, u):
                nc.gpsimd.tensor_copy(idx_now[:, u, :], s_idx[order][:, bass.ds(r * SLOTS, SLOTS)]).then_inc(idx_ready, 1)
                pool.wait_ge(idx_ready, r + (phase * ROUNDS + 1))

            def gather(table, to, u, b):
                nc.gpsimd.indirect_dma_start(
                    out=to, out_offset=None, in_=table[:, :],
                    in_offset=bass.IndirectOffsetOnAxis(ap=idx_now[:, u, b:b + 1], axis=0),
                ).then_inc(gathered[b], 16)

            def gather_layer0(phase, order, table):
                def turn(r, u):
                    round_indices(phase, order, r, u)
                    for b in range(SLOTS):
                        pool.wait_ge(chunks_summed, r * SLOTS + (phase * CHUNKS + b + 1))
                        pool.nop(nofuse=True)
                        gather(table, rows0[:, b, :], u, b)

                turn(0, phase % 2)
                with pool.Fori(0, ROUNDS // 2) as i:
                    for u in range(2):
                        turn(i * 2 + (u + 1), (phase + u + 1) % 2)

            def gather_layer1(o, table, width):
                phase = 1 + int(o)

                def to(b):
                    return row_slots(b, 1)[:, 0, 0:width]

                round_indices(phase, "S", 0, phase % 2)
                for b in range(SLOTS):
                    gather(table, to(b), phase % 2, b)
                with pool.Fori(0, ROUNDS // 2) as i:
                    for u in range(2):
                        r, side = i * 2 + (u + 1), (phase + u + 1) % 2
                        round_indices(phase, "S", r, side)
                        for b in range(SLOTS):
                            pool.wait_ge(msg_ready[o], r * SLOTS + (b + 1 - SLOTS))
                            pool.nop(nofuse=True)
                            gather(table, to(b), side, b)

            pool.wait_ge(q_zero, 16)
            pool.wait_ge(rec_ready, 1)

            def scatter(r, u, first):
                if not first:
                    pool.wait_ge(scattered[u], r * (8 * SLOTS) - u * (8 * SLOTS))
                nc.gpsimd.tensor_copy(rec_now[:, u, :, :].rearrange("p c f -> p (c f)"),
                                      rec[:, bass.ds(r * SLOTS, SLOTS), :].rearrange("p c f -> p (c f)")).then_inc(rec_staged, 1)
                nc.gpsimd.tensor_copy(idx_now[:, u, :], rec_row[:, bass.ds(r * SLOTS, SLOTS)]).then_inc(rec_staged, 1)
                pool.wait_ge(rec_staged, r * 2 + 2)
                pool.nop(nofuse=True)
                for b in range(SLOTS):
                    nc.gpsimd.indirect_dma_start(
                        out=records[:, :], out_offset=bass.IndirectOffsetOnAxis(ap=idx_now[:, u, b:b + 1], axis=0),
                        in_=rec_now[:, u, b, :], in_offset=None).then_inc(scattered[u], 16)

            for u in range(2):
                scatter(u, u, True)
            with pool.Fori(1, SORT_ROUNDS // 2) as i:
                for u in range(2):
                    scatter(i * 2 + u, u, False)

            for u in range(2):
                pool.wait_ge(scattered[u], 16 * SLOTS * (SORT_ROUNDS // 2))
            pool.wait_ge(edges_sorted, 1)
            pool.wait_ge(tab_ab, 32)
            gather_layer0(0, "S", table_a)
            pool.wait_ge(q_by_dst, 16)
            gather_layer0(1, "D", table_b)
            pool.wait_ge(tab_1[0], 16 * ((T + 1) // 2))
            pool.wait_ge(tab_1[1], 16 * (T // 2))
            gather_layer1("1", table_1, W1)
            pool.wait_ge(tab_2[0], 16 * ((T + 1) // 2))
            pool.wait_ge(tab_2[1], 16 * (T // 2))
            gather_layer1("2", table_2, W2)

        @block.scalar
        def _(act):
            def normalise(round_):
                act.wait_ge(moments_ready, T * (round_ + 1))
                nc.scalar.activation(rstd[:, :], mv[:, :, 1], ACT.Sqrt, bias=eps[:, :]).then_inc(std_ready, 1)
                act.wait_ge(nb_ready, round_ + 1)
                for t in range(T):
                    nc.scalar.activation(norm[:, t, :], xs[:, t, :], ACT.Relu, bias=nbias[:, t:t + 1],
                                         scale=rstd[:, t:t + 1]).then_inc(normed, 1)

            with act.Fori(0, SORT_ROUNDS) as i:
                for k in range(SLOTS):
                    c, slot = i * SLOTS + k, k % RING
                    act.wait_ge(lane_ready, c + 1)
                    for to, by in ((oh_w[:, slot, 1, :], w_part[:, 1, bass.ds(c, 1)]), (oh_w[:, slot, 2, :], w_part[:, 2, bass.ds(c, 1)]),
                                   (oh_i2[:, slot, :], index[:, 1, bass.ds(c, 1)])):
                        last = nc.scalar.activation(to, oh_lane[:, slot, :], ACT.Copy, scale=by)
                    last.then_inc(fields_ready, 1)

            normalise(0)
            act.wait_ge(l0_done, 1)
            normalise(1)

            def dense(o, width, landed):
                for t in range(T + 1):
                    if t < T:
                        act.wait_ge(featT_psum[o], t + 1)
                        if t >= 2:
                            act.wait_ge(dense_psum[o], t - 1)
                        nk = width_in[o]
                        nc.scalar.copy(featT[:, t % 2, 0:nk], bank[t % 2][:, 0:nk]).then_inc(featT_ready[o], 1)
                    if t >= 1:
                        u = t - 1
                        act.wait_ge(dense_psum[o], u + 1)
                        if u >= 2:
                            act.wait_ge(landed[u % 2], 16 * (u // 2))
                        nc.scalar.copy(stage[:, u % 2, 0:width], bank[2 + u % 2][:, 0:width]).then_inc(dense_act[o], 1)

            def attend(o):
                heads = HEADS if o == "1" else 1

                def transposed(q, u):
                    act.wait_ge(ohT_psum[o], q + 1)
                    nc.scalar.activation(ohT[:, u % 2, :], bank[u % 2][:, :], ACT.Copy).then_inc(ohT_ready[o], 1)

                def weights(q, u):
                    act.wait_ge(lrelu_ready[o], q + 1)
                    nc.scalar.activation(e_att[:, u % 2, 0:QUAD * heads], lrelu[:, u % 2, 0:QUAD * heads], ACT.Exp,
                                         scale=-1.0).then_inc(e_ready[o], 1)

                def turn(i):
                    for u in range(UNROLL):
                        q = i * UNROLL + u
                        if not isinstance(i, int) or q + 2 < QUADS:
                            transposed(i * UNROLL + (u + 2), u)
                        if not isinstance(i, int) or q + 1 < QUADS:
                            weights(i * UNROLL + (u + 1), u + 1)

                transposed(0, 0)
                transposed(1, 1)
                weights(0, 0)
                turn(0)
                with act.Fori(1, ROUNDS - 1) as i:
                    turn(i)
                turn(ROUNDS - 1)

            width_in = {"1": C, "2": HD}
            dense("1", HD, tab_1)
            attend("1")
            act.wait_ge(var_ready, 1)
            nc.scalar.activation(head_var[:, :, :], head_var[:, :, :], ACT.Sqrt, bias=eps[:, :], scale=1.0 / D).then_inc(std_ready, 1)
            for t in range(T):
                act.wait_ge(elu_in, t + 1)
                nc.scalar.activation(neg[:, t % 2, :], neg[:, t % 2, :], ACT.Exp).then_inc(elu_out, 1)
            dense("2", C, tab_2)
            attend("2")
            act.wait_ge(var_ready, 2)
            nc.scalar.activation(rstd[:, :], mv[:, :, 1], ACT.Sqrt, bias=eps[:, :]).then_inc(std_ready, 1)
            for t in range(T):
                act.wait_ge(elu2_in, t + 1)
                nc.scalar.activation(neg[:, t % 2, 0:C], neg[:, t % 2, 0:C], ACT.Exp).then_inc(elu2_out, 1)

        @block.tensor
        def _(pe):
            pe.wait_ge(consts_made, 1)
            pe.wait_ge(q_weights, 16 * 11)
            for k in range(4):
                for m in range(2):
                    nc.tensor.transpose(bank[m][:, k * P:(k + 1) * P], wh[:, k, m * P:(m + 1) * P], ident[:, :])
            for k in range(2):
                for m in range(4):
                    b = bank[2 + m // 2][:, (m % 2) * C + k * P:(m % 2) * C + (k + 1) * P]
                    nc.tensor.transpose(b, wo[:, k, m * P:(m + 1) * P], ident[:, :])
            for m in range(2):
                for k in range(4):
                    nc.tensor.matmul(bank[4][:, m * 16:m * 16 + 16], wh[:, k, m * P:(m + 1) * P],
                                     ah[:, k * 16:(k + 1) * 16], start=(k == 0), stop=(k == 3))
            for m in range(4):
                for k in range(2):
                    nc.tensor.matmul(bank[4][:, 32 + 2 * m:34 + 2 * m], wo[:, k, m * P:(m + 1) * P],
                                     ao[:, k:k + 3:2], start=(k == 0), stop=(k == 1))
            for k in range(4):
                nc.tensor.matmul(bank[5][0:1, 0:16], bh_col[:, k:k + 1], ah[:, k * 16:(k + 1) * 16],
                                 start=(k == 0), stop=(k == 3))
            for k in range(2):
                last = nc.tensor.matmul(bank[5][0:1, 16:18], bo_col[:, k:k + 1], ao[:, k:k + 3:2],
                                        start=(k == 0), stop=(k == 1))
            last.then_inc(pe_chain, 1)

            def prefix(n):
                pe.wait_ge(counted, n + 1)
                nc.tensor.matmul(bank[6][:, 0:T], before[:, :], count[:, :], start=True, stop=True)
                nc.tensor.matmul(bank[7][:, 0:T], ones[:, 0:P], count[:, :], start=True, stop=True).then_inc(offsets, 1)

            def sort_place(slot, start, stop):
                lhs = [oh_w[:, slot, f, :] for f in range(3)] + [oh_i1[:, slot, :], oh_i2[:, slot, :]]
                for b in range(5):
                    last = nc.tensor.matmul(bank[b][:, 0:CHUNKS], lhs[b], oh_chunk[:, slot, :], start=start, stop=stop)
                last.then_inc(col_free, 1)

            def sort_round(i, at_start=False, at_end=False):
                for k in range(SLOTS):
                    pe.wait_ge(col_ready, i * SLOTS + (k + 1))
                    pe.wait_ge(fields_ready, i * SLOTS + (k + 1))
                    sort_place(k % RING, at_start and k == 0, at_end and k == SLOTS - 1)

            def sum_rows(o, phase, i, k):
                c = i * SLOTS + k
                g = i * (SLOTS // GP) + k // GP
                if k % GP == 0:
                    pe.wait_ge(sum_free[o], g + 1)
                pe.wait_ge(oh_ready[o], c + 1)
                pe.wait_ge(gathered[k], i * 16 + 16 * (phase * ROUNDS + 1))
                b = bank[4 + (k // GP) % 4]
                nc.tensor.matmul(b[:, 0:HALF], oh[:, k, :], rows0[:, k, :], start=(k % GP == 0), stop=False)
                nc.tensor.matmul(b[:, HALF:HALF + 1], oh_count[:, k, :], one_b[:, :], start=False,
                                 stop=(k % GP == GP - 1)).then_inc(chunks_summed, 1)

            prefix(0)
            prefix(1)
            pe.wait_ge(w_evac, 1)
            sort_round(0, at_start=True)
            with pe.Fori(1, SORT_ROUNDS - 1) as i:
                sort_round(i)
            sort_round(SORT_ROUNDS - 1, at_end=True)
            last = None
            for o, phase in (("S", 0), ("D", 1)):
                with pe.Fori(0, ROUNDS) as i:
                    for k in range(SLOTS):
                        sum_rows(o, phase, i, k)

            def dense(o, nk, width, rhs, rhs_s, b_row, b_s, ns, feats_ready, feat):
                for t in range(T + 1):
                    if t < T:
                        feats_ready(t)
                        if t >= 2:
                            pe.wait_ge(featT_ready[o], t - 1)
                        for k in range(nk):
                            last = nc.tensor.transpose(bank[t % 2][:, k * P:(k + 1) * P], feat[:, t, k * P:(k + 1) * P], ident[:, :])
                        last.then_inc(featT_psum[o], 1)
                    if t >= 1:
                        u = t - 1
                        pe.wait_ge(featT_ready[o], u + 1)
                        if u >= 2:
                            pe.wait_ge(dense_act[o], u - 1)
                            pe.wait_ge(dense_dve[o], u - 1)
                        nc.tensor.matmul(bank[2 + u % 2][:, 0:width], ones[0:1, 0:P], b_row[0:1, :], start=True, stop=False)
                        for k in range(nk):
                            nc.tensor.matmul(bank[2 + u % 2][:, 0:width], featT[:, u % 2, k * P:(k + 1) * P], rhs[:, k, :],
                                             start=False, stop=(k == nk - 1))
                        nc.tensor.matmul(bank[4 + u % 2][:, 0:ns], ones[0:1, 0:P], b_s[0:1, :], start=True, stop=False)
                        for k in range(nk):
                            last = nc.tensor.matmul(bank[4 + u % 2][:, 0:ns], featT[:, u % 2, k * P:(k + 1) * P], rhs_s[:, k, :],
                                                    start=False, stop=(k == nk - 1))
                        last.then_inc(dense_psum[o], 1)

            def attend(o):
                heads, width, s_src = (HEADS, HD, s_src1) if o == "1" else (1, C, s_src2)

                def transposed(q, u):
                    pe.wait_ge(oh_ready[o], q + 1)
                    for k in range(QUAD):
                        last = nc.tensor.transpose(bank[u % 2][:, k * P:(k + 1) * P], oh[:, u % UNROLL * QUAD + k, :], ident[:, :])
                    last.then_inc(ohT_psum[o], 1)

                def source_scores(q, u, tiles):
                    pe.wait_ge(ohT_ready[o], q + 1)
                    for k in range(QUAD):
                        last = nc.tensor.matmul(bank[2 + u % 2][:, k * heads:(k + 1) * heads], ohT[:, u % 2, k * P:(k + 1) * P],
                                                s_src[:, bass.ds(tiles[k // 2], 1), :].rearrange("p t h -> p (t h)"),
                                                start=True, stop=True)
                    last.then_inc(ssrc_ready[o], 1)

                def sums(q, u):
                    for k in range(QUAD):
                        if k % GP == 0:
                            pe.wait_ge(sum_free[o], q * 2 + (k // GP + 1))
                        pe.wait_ge(msg_ready[o], q * QUAD + (k + 1))
                        mm = nc.tensor.matmul(bank[4 + u % 2 * 2 + k // GP][:, 0:width], oh[:, u * QUAD + k, :],
                                              msg[:, u % 2 * QUAD + k, 0:width], start=(k % GP == 0), stop=(k % GP == GP - 1))
                        if k % GP == GP - 1:
                            mm.then_inc(sum_ready[o], 1)

                def turn(i):
                    n = 2 * UNROLL if not isinstance(i, int) or i < ROUNDS - 1 else 2 * UNROLL - 2
                    tiles = tile_numbers(mybir.EngineType.PE, "S", i * (2 * UNROLL) + (TILE_AT + 2), n)
                    for u in range(UNROLL):
                        q = i * UNROLL + u
                        if not isinstance(i, int) or q + 1 < QUADS:
                            source_scores(i * UNROLL + (u + 1), u + 1, tiles[2 * u:2 * u + 2])
                        sums(q, u)
                        if not isinstance(i, int) or q + 2 < QUADS:
                            transposed(i * UNROLL + (u + 2), u + 2)

                transposed(0, 0)
                transposed(1, 1)
                source_scores(0, 0, tile_numbers(mybir.EngineType.PE, "S", TILE_AT, 2))
                turn(0)
                with pe.Fori(1, ROUNDS - 1) as i:
                    turn(i)
                turn(ROUNDS - 1)

            dense("1", 2, HD, whT, ahT, bh_row, bah, 2 * HEADS, lambda t: pe.wait_ge(normed, T + t + 1), norm)
            pe.wait_ge(dense_act["1"], T)
            pe.wait_ge(dense_dve["1"], T)
            attend("1")
            dense("2", 4, C, woT, aoT, bo_row, bao, 2, lambda t: pe.wait_ge(z_done, t + 1), work)
            pe.wait_ge(dense_act["2"], T)
            pe.wait_ge(dense_dve["2"], T)
            attend("2")

        @block.vector
        def _(dve):
            v = nc.vector
            linked = [0]

            def link(ins):
                linked[0] += 1
                ins.then_inc(dve_chain, 1)
                dve.wait_ge(dve_chain, linked[0])

            v.memset(nat["src"][:, :], T * P).then_inc(q_pad, 1)
            v.memset(nat["dst"][:, :], T * P).then_inc(q_pad, 1)
            v.memset(nat_w[:, :], 0.0).then_inc(q_pad, 1)
            v.memset(ah[:, :], 0.0)
            v.memset(work[:, :, C:HD], 0.0).then_inc(acc_zeroed, 1)
            v.memset(xs[:, T - 1, :], 0.0).then_inc(q_pad, 1)
            v.memset(ones[:, :], 1.0)
            v.memset(eps[:, :], EPS)
            v.memset(one_b[:, :], 1.0)
            for o in "SD":
                v.memset(group_tile[o][0:1, 0:TILE_AT], 0)
            dve.wait_ge(iota_made, 2)
            link(v.tensor_copy(iota_f[:, :], iota_i[:, :]))
            link(v.tensor_copy(row_f[:, :], row_i[:, :]))
            v.tensor_copy(iota_lane[:, :], iota_i[:, 0:P])
            v.tensor_copy(iota_chunk[:, :], iota_i[:, 0:CHUNKS])
            v.tensor_scalar(ident[:, :], iota_f[:, 0:P], row_f[:, :], None, ALU.is_equal)
            link(v.tensor_scalar(before[:, :], iota_f[:, 0:P], row_f[:, :], None, ALU.is_gt))
            dve.sem_inc(consts_made, 1)
            dve.sem_inc(chunks_summed, SLOTS)
            dve.sem_inc(col_free, RING)
            for o in "SD":
                dve.sem_inc(sum_free[o], 4)

            def tile_statistics(t):
                v.bn_stats(stats[:, bass.ds(t, 1), :].rearrange("p t c -> p (t c)"),
                           xs[:, bass.ds(t, 1), :].rearrange("p t c -> p (t c)")).then_inc(stats_ready, 1)

            def tile_moments(t, before):
                dve.wait_ge(stats_ready, t + (before + 1))
                v.bn_aggr(mv[:, t, :], stats[:, t, :]).then_inc(moments_ready, 1)

            def scales(round_):
                dve.wait_ge(std_ready, round_ + 1)
                link(v.reciprocal(rstd[:, :], rstd[:, :]))
                v.scalar_tensor_tensor(out=nbias[:, :], in0=mv[:, :, 0], scalar=-1.0, in1=rstd[:, :],
                                       op0=ALU.mult, op1=ALU.mult).then_inc(nb_ready, 1)

            def positions(o, n, key):
                link(v.tensor_scalar(lo_i[:, :], key[:, :], P - 1, None, ALU.bitwise_and))
                link(v.tensor_copy(key_lo[:, :], lo_i[:, :]))
                link(v.tensor_scalar(lo_i[:, :], key[:, :], 7, None, ALU.logical_shift_right))
                link(v.tensor_copy(tile_f[:, :], lo_i[:, :]))
                for t in range(T):
                    last = v.tensor_scalar(in_tile[:, t, :], tile_f[:, :], float(t), 0.0, ALU.is_equal, ALU.add,
                                           accum_out=count[:, t:t + 1])
                last.then_inc(counted, 1)
                dve.wait_ge(offsets, n + 1)
                link(v.tensor_scalar(cap[:, :], bank[7][:, 0:T], float(GP * P - 1), None, ALU.add))
                link(v.tensor_copy(cap_i[:, :], cap[:, :]))
                link(v.tensor_scalar(cap_i[:, :], cap_i[:, :], 8, None, ALU.logical_shift_right))
                link(v.tensor_copy(cap[:, :], cap_i[:, :]))
                link(v.tensor_tensor_scan(cap_sum[:, :], ones[:, 0:T], cap[:, :], 0.0, ALU.mult, ALU.add))
                link(v.tensor_sub(first[:, :], cap_sum[:, :], cap[:, :]))
                link(v.scalar_tensor_tensor(out=first[:, :], in0=first[:, :], scalar=float(GP * P), in1=bank[6][:, 0:T],
                                            op0=ALU.mult, op1=ALU.add))
                link(v.tensor_tensor(below[0:1, :, :], cap_sum[0:1, :].unsqueeze(1).to_broadcast([1, GROUPS, T]),
                                     iota_f[0:1, 0:GROUPS].unsqueeze(2).to_broadcast([1, GROUPS, T]), ALU.is_le))
                link(v.tensor_reduce(tile_sum[0:1, :], below[0:1, :, :], AX.X, ALU.add))
                link(v.tensor_scalar(tile_sum[0:1, :], tile_sum[0:1, :], float(T - 1), None, ALU.min))
                link(v.tensor_copy(group_tile[o][0:1, TILE_AT:], tile_sum[0:1, :]))
                link(v.tensor_scalar(pos[:, :], iota_f[:, 0:COLS], float(P * CHUNKS + 1), None, ALU.add))
                for t in range(T):
                    link(v.tensor_tensor_scan(rank[:, t % 2, :], ones[:, :], in_tile[:, t, :], first[:, t:t + 1], ALU.mult, ALU.add))
                    last = v.copy_predicated(pos[:, :], in_tile[:, t, :].bitcast(U16), rank[:, t % 2, :])
                link(last)
                link(v.tensor_scalar(pos[:, :], pos[:, :], -1.0, None, ALU.add))
                link(v.tensor_copy(pos_i[:, :], pos[:, :]))
                link(v.tensor_scalar(lo_i[:, :], pos_i[:, :], P - 1, None, ALU.bitwise_and))
                link(v.tensor_copy(lane[:, :], lo_i[:, :]))
                link(v.tensor_scalar(lo_i[:, :], pos_i[:, :], 7, None, ALU.logical_shift_right))
                link(v.tensor_copy(chunk[:, :], lo_i[:, :]))

            def records_by_dst():
                v.tensor_copy(rec[:, :, 0], nat_w)
                v.tensor_copy(rec[:, :, 1].bitcast(I32), nat["src"])
                v.tensor_copy(rec[:, :, 2], key_lo)
                v.memset(rec[:, :, 3], 1.0)
                link(v.scalar_tensor_tensor(out=pos[:, :], in0=lane, scalar=float(PITCH), in1=chunk, op0=ALU.mult, op1=ALU.add))
                v.tensor_copy(rec_row, pos[:, :]).then_inc(rec_ready, 1)

            def fields_by_src():
                link(v.tensor_copy(w_b[:, :], nat_w[:, :]))
                link(v.tensor_copy(w_part[:, 0, :], w_b[:, :]))
                link(v.tensor_sub(tile_f[:, :], nat_w[:, :], w_part[:, 0, :]))
                link(v.tensor_copy(w_b[:, :], tile_f[:, :]))
                link(v.tensor_copy(w_part[:, 1, :], w_b[:, :]))
                link(v.tensor_sub(w_part[:, 2, :], tile_f[:, :], w_part[:, 1, :]))
                link(v.tensor_scalar(lo_i[:, :], nat["dst"], 1, None, ALU.logical_shift_right))
                link(v.tensor_copy(index[:, 0, :], lo_i[:, :]))
                link(v.tensor_scalar(lo_i[:, :], nat["dst"], 1, None, ALU.bitwise_and))
                link(v.tensor_copy(index[:, 1, :], lo_i[:, :]))
                link(v.scalar_tensor_tensor(out=index[:, 1, :], in0=index[:, 1, :], scalar=float(P), in1=key_lo,
                                            op0=ALU.mult, op1=ALU.add))
                link(v.tensor_scalar(index[:, 1, :], index[:, 1, :], 1.0, None, ALU.add))

            def sort_column(c, slot):
                dve.wait_ge(col_free, c + 1)
                at = lane[:, bass.ds(c, 1)]
                v.tensor_scalar(oh_lane[:, slot, :], iota_lane[:, :], at, None, ALU.is_equal).then_inc(lane_ready, 1)
                v.tensor_scalar(oh_chunk[:, slot, :], iota_chunk[:, :], chunk[:, bass.ds(c, 1)], None, ALU.is_equal)
                v.tensor_scalar(oh_w[:, slot, 0, :], iota_lane[:, :], at, w_part[:, 0, bass.ds(c, 1)], ALU.is_equal, ALU.mult)
                v.tensor_scalar(oh_i1[:, slot, :], iota_lane[:, :], at, index[:, 0, bass.ds(c, 1)], ALU.is_equal,
                                ALU.mult).then_inc(col_ready, 1)

            def edges_by_src():
                dve.wait_ge(col_free, RING + COLS)
                link(v.tensor_scalar(s_lo["S"][:, :], bank[4][:, 0:CHUNKS], -1.0, None, ALU.add))
                link(v.tensor_scalar(s_odd[:, :], s_lo["S"][:, :], float(P), None, ALU.is_ge))
                link(v.scalar_tensor_tensor(out=s_idx["S"][:, :], in0=bank[3][:, 0:CHUNKS], scalar=2.0, in1=s_odd[:, :],
                                            op0=ALU.mult, op1=ALU.add))
                v.scalar_tensor_tensor(out=s_lo["S"][:, :], in0=s_odd[:, :], scalar=-float(P), in1=s_lo["S"][:, :],
                                       op0=ALU.mult, op1=ALU.add)
                link(v.tensor_copy(s_w["S"][:, :], bank[0][:, 0:CHUNKS]))
                link(v.tensor_add(s_w["S"][:, :], s_w["S"][:, :], bank[1][:, 0:CHUNKS]))
                link(v.tensor_add(s_w["S"][:, :], s_w["S"][:, :], bank[2][:, 0:CHUNKS]))
                dve.sem_inc(edges_sorted, 1)

            def weighted_one_hot(o, phase, i, k):
                c = i * SLOTS + k
                dve.wait_ge(chunks_summed, c + (phase * CHUNKS + 1))
                v.tensor_scalar(oh_count[:, k, :], iota_lane[:, :], s_lo[o][:, bass.ds(c, 1)], None, ALU.is_equal)
                v.tensor_scalar(oh[:, k, :], iota_f[:, 0:P], s_lo[o][:, bass.ds(c, 1)], s_w[o][:, bass.ds(c, 1)],
                                ALU.is_equal, ALU.mult).then_inc(oh_ready[o], 1)

            def add_group(o, acc, tile, g, psum, banks):
                dve.wait_ge(sum_free[o], g + banks)
                a = acc[:, bass.ds(tile, 1), :].rearrange("p t c -> p (t c)")
                v.tensor_add(a, a, psum).then_inc(sum_free[o], 1)

            def layer0(o, phase):
                def add(i, j, tile):
                    g = i * (SLOTS // GP) + j
                    dve.wait_ge(chunks_summed, i * SLOTS + (SLOTS + phase * CHUNKS + GP * j + GP))
                    add_group(o, acc[o], tile, g, bank[4 + j % 4][:, 0:HALF + 1], 4)

                def turn(i):
                    tiles = tile_numbers(mybir.EngineType.DVE, o, i * (SLOTS // GP) + (TILE_AT - 2), SLOTS // GP)
                    for k in range(SLOTS):
                        weighted_one_hot(o, phase, i, k)
                        j = k // GP
                        if k % GP == GP - 1 and (j >= 2 or not isinstance(i, int)):
                            add(i, j - 2, tiles[j])

                turn(0)
                with dve.Fori(1, ROUNDS) as i:
                    turn(i)
                tiles = tile_numbers(mybir.EngineType.DVE, o, TILE_AT + GROUPS - 2, 2)
                for j in range(2):
                    add(ROUNDS - 1, SLOTS // GP - 2 + j, tiles[j])
                dve.wait_ge(sum_free[o], GROUPS + 4)

            def add_means(o, half):
                link(v.tensor_scalar(rdeg[:, :, :], acc[o][:, :, HALF:HALF + 1], 1.0, None, ALU.max))
                link(v.reciprocal(rdeg[:, :, :], rdeg[:, :, :]))
                mean = acc[o][:, :, 0:HALF]
                link(v.tensor_tensor(mean, mean, rdeg[:, :, :].to_broadcast([P, T, HALF]), ALU.mult))
                link(v.tensor_tensor(half, half, mean, ALU.add))

            dve.wait_ge(q_edges, 96)
            positions("D", 0, nat["dst"])
            records_by_dst()
            positions("S", 1, nat["src"])
            fields_by_src()

            dve.wait_ge(pe_chain, 1)
            for m in range(2):
                v.tensor_copy(whT[:, m, :], bank[m][:, :])
                v.tensor_copy(woT[:, 2 * m:2 * m + 2, :].rearrange("p k c -> p (k c)"), bank[2 + m][:, :])
            v.tensor_copy(ahT[:, :, :].rearrange("p k c -> p (k c)"), bank[4][:, 0:32])
            v.tensor_copy(aoT[:, :, :].rearrange("p k c -> p (k c)"), bank[4][:, 32:40])
            v.tensor_copy(bah[0:1, :], bank[5][0:1, 0:16])
            v.tensor_copy(bao[0:1, :], bank[5][0:1, 16:18]).then_inc(w_evac, 1)

            dve.wait_ge(q_x, 32)
            with dve.Fori(0, T) as i:
                tile_statistics(i)
                for k in range(SLOTS):
                    sort_column(i * SLOTS + k, k % RING)
            for k in range(SLOTS * (SORT_ROUNDS - T)):
                sort_column(T * SLOTS + k, k % RING)
            for t in range(T):
                tile_moments(t, 0)
            scales(0)
            edges_by_src()

            layer0("S", 0)
            dve.wait_ge(tab_ab, 32)
            link(v.memset(acc["D"], 0.0))
            dve.wait_ge(q_by_dst, 16)
            link(v.tensor_tensor(s_lo["D"], s_lo["D"], by_dst[:, :, 3], ALU.add))
            link(v.tensor_scalar(s_lo["D"], s_lo["D"], -1.0, None, ALU.add))
            add_means("S", xs[:, :, 0:HALF])
            layer0("D", 1)
            add_means("D", xs[:, :, HALF:C])
            dve.sem_inc(l0_done, 1)
            for t in range(T):
                tile_statistics(t)
            for t in range(T):
                tile_moments(t, T)
            scales(1)

            def dense(o, width, ns, s_src, landed):
                for t in range(T):
                    dve.wait_ge(dense_psum[o], t + 1)
                    if t >= 2:
                        dve.wait_ge(landed[t % 2], 16 * (t // 2))
                    v.tensor_copy(s_src[:, t, :], bank[4 + t % 2][:, 0:ns])
                    v.tensor_copy(stage[:, t % 2, width:width + ns], bank[4 + t % 2][:, ns:2 * ns]).then_inc(dense_dve[o], 1)

            def attend(o):
                heads, width = (HEADS, HD) if o == "1" else (1, C)
                acc = work[:, :, 0:width]
                dve.sem_inc(sum_free[o], 4)

                def one_hots(q, u):
                    for k in range(QUAD):
                        last = v.tensor_scalar(oh[:, u % UNROLL * QUAD + k, :], iota_f[:, 0:P],
                                               s_lo["S"][:, bass.ds(q * QUAD + k, 1)], None, ALU.is_equal)
                    last.then_inc(oh_ready[o], 1)

                def scores(i, q, u):
                    n = QUAD * heads
                    dve.wait_ge(ssrc_ready[o], q + 1)
                    for k in range(QUAD):
                        b = u % UNROLL * QUAD + k
                        dve.wait_ge(gathered[b], i * 16 + 16 * ((1 + int(o)) * ROUNDS + 1 + u // UNROLL))
                    v.tensor_tensor(score[:, u % 2, 0:n].rearrange("p (k h) -> p k h", h=heads),
                                    bank[2 + u % 2][:, 0:n].rearrange("p (k h) -> p k h", h=heads),
                                    row_slots(u % UNROLL * QUAD, QUAD)[:, :, width:width + heads], ALU.add).then_inc(z_ready[o], 1)
                    dve.wait_ge(z_ready[o], q + 1)
                    v.scalar_tensor_tensor(out=lrelu[:, u % 2, 0:n], in0=score[:, u % 2, 0:n], scalar=ALPHA,
                                           in1=score[:, u % 2, 0:n], op0=ALU.mult, op1=ALU.max).then_inc(lrelu_ready[o], 1)

                def messages(q, u):
                    dve.wait_ge(e_ready[o], q + 1)
                    for k in range(QUAD):
                        row = row_slots(u * QUAD + k, 1)[:, 0, 0:width]
                        e, m = e_att[:, u % 2, k * heads:(k + 1) * heads], msg[:, u % 2 * QUAD + k, 0:width]
                        if heads == 1:
                            ins = v.tensor_scalar(m, row, e, None, ALU.mult)
                        else:
                            ins = v.tensor_tensor(m.rearrange("p (h d) -> p h d", h=heads),
                                                  row.rearrange("p (h d) -> p h d", h=heads),
                                                  e.unsqueeze(2).to_broadcast([P, heads, D]), ALU.mult)
                        ins.then_inc(msg_ready[o], 1)

                def add_groups(q, u, tiles):
                    for j in range(2):
                        dve.wait_ge(sum_ready[o], q * 2 + (j + 1))
                        add_group(o, acc, tiles[j], q * 2 + j, bank[4 + u % 2 * 2 + j][:, 0:width], 4)

                def turn(i):
                    tiles = tile_numbers(mybir.EngineType.DVE, "S", i * (2 * UNROLL) + (TILE_AT - 2), 2 * UNROLL)
                    for u in range(UNROLL):
                        q, static = i * UNROLL + u, isinstance(i, int)
                        messages(q, u)
                        if not static or q + 2 < QUADS:
                            one_hots(i * UNROLL + (u + 2), u + 2)
                        if not static or q + 1 < QUADS:
                            scores(i, i * UNROLL + (u + 1), u + 1)
                        if not static or q >= 1:
                            add_groups(i * UNROLL + (u - 1), u - 1, tiles[2 * u:2 * u + 2])

                one_hots(0, 0)
                one_hots(1, 1)
                scores(0, 0, 0)
                turn(0)
                with dve.Fori(1, ROUNDS - 1) as i:
                    turn(i)
                turn(ROUNDS - 1)
                add_groups(QUADS - 1, UNROLL - 1, tile_numbers(mybir.EngineType.DVE, "S", TILE_AT + GROUPS - 2, 2))

            dense("1", HD, HEADS, s_src1, tab_1)
            link(v.memset(work[:, :, :], 0.0))
            attend("1")
            dve.wait_ge(sum_free["1"], GROUPS + 4)

            dve.wait_ge(q_gains, 64)
            def per_head(a):
                return a.rearrange("p (h d) -> p h d", h=HEADS)

            for t in range(T):
                last = v.tensor_reduce(head_mean[:, t, :], per_head(work[:, t, :]), AX.X, ALU.add)
            link(last)
            link(v.tensor_scalar(head_mean[:, :, :], head_mean[:, :, :], 1.0 / D, None, ALU.mult))
            for t in range(T):
                y = per_head(work[:, t, :])
                link(v.tensor_tensor(y, y, head_mean[:, t, :].unsqueeze(2).to_broadcast([P, HEADS, D]), ALU.subtract))
                link(v.tensor_tensor(tmp[:, t % 2, :], work[:, t, :], work[:, t, :], ALU.mult))
                last = v.tensor_reduce(head_var[:, t, :], per_head(tmp[:, t % 2, :]), AX.X, ALU.add)
            last.then_inc(var_ready, 1)
            dve.wait_ge(std_ready, 3)
            link(v.reciprocal(head_var[:, :, :], head_var[:, :, :]))
            for t in range(T):
                y = per_head(work[:, t, :])
                link(v.tensor_tensor(y, y, head_var[:, t, :].unsqueeze(2).to_broadcast([P, HEADS, D]), ALU.mult))
                link(v.tensor_tensor(work[:, t, :], work[:, t, :], gh[:, :], ALU.mult))
                link(v.tensor_tensor(work[:, t, :], work[:, t, :], betah[:, :], ALU.add))
                v.tensor_scalar(neg[:, t % 2, :], work[:, t, :], 0.0, None, ALU.min).then_inc(elu_in, 1)
                link(v.tensor_scalar(pose[:, t % 2, :], work[:, t, :], 0.0, None, ALU.max))
                dve.wait_ge(elu_out, t + 1)
                v.scalar_tensor_tensor(out=work[:, t, :], in0=neg[:, t % 2, :], scalar=-1.0, in1=pose[:, t % 2, :],
                                       op0=ALU.add, op1=ALU.add).then_inc(z_done, 1)

            dense("2", C, 1, s_src2, tab_2)
            link(v.memset(work[:, :, 0:C], 0.0))
            attend("2")
            dve.wait_ge(sum_free["2"], GROUPS + 4)

            for t in range(T):
                link(v.bn_stats(stats[:, t, :], work[:, t, 0:C]))
                last = v.bn_aggr(mv[:, t, :], stats[:, t, :])
            last.then_inc(var_ready, 1)
            dve.wait_ge(std_ready, 4)
            link(v.reciprocal(rstd[:, :], rstd[:, :]))
            for t in range(T):
                y = work[:, t, 0:C]
                link(v.tensor_scalar(y, y, mv[:, t, 0:1], rstd[:, t:t + 1], ALU.subtract, ALU.mult))
                link(v.tensor_tensor(y, y, go[:, :], ALU.mult))
                link(v.tensor_tensor(y, y, betao[:, :], ALU.add))
                v.tensor_scalar(neg[:, t % 2, 0:C], y, 0.0, None, ALU.min).then_inc(elu2_in, 1)
                link(v.tensor_scalar(pose[:, t % 2, 0:C], y, 0.0, None, ALU.max))
                link(v.tensor_tensor(pose[:, t % 2, 0:C], pose[:, t % 2, 0:C], xs[:, t, :], ALU.add))
                dve.wait_ge(elu2_out, t + 1)
                if t >= 2:
                    dve.wait_ge(q_out[t % 2], 16 * (t // 2))
                v.scalar_tensor_tensor(out=final[:, t % 2, :], in0=neg[:, t % 2, 0:C], scalar=-1.0, in1=pose[:, t % 2, 0:C],
                                       op0=ALU.add, op1=ALU.add).then_inc(final_ready, 1)


_INS = ["x", "src", "dst", "edge_weight", "L1_gnn_W_heads", "L1_gnn_b_heads", "L1_gnn_a_heads", "L1_gnn_g_heads",
        "L1_gnn_beta_heads", "L1_gnn_W_out", "L1_gnn_b_out", "L1_gnn_a_out", "L1_gnn_g_out", "L1_gnn_beta_out"]


def kernel(**inputs):
    import numpy as _np
    import concourse.bacc as _bacc
    from concourse import mybir as _mybir
    from concourse.bass_utils import run_bass_kernel_spmd as _run

    nc = _bacc.Bacc("TRN2", target_bir_lowering=False, num_devices=1)
    arrays, args = {}, []
    for name in _INS:
        a = _np.ascontiguousarray(inputs[name])
        arrays[f"in_{name}"] = a
        args.append(nc.dram_tensor(f"in_{name}", a.shape, _mybir.dt.from_np(a.dtype), kind="ExternalInput").ap())
    args.append(nc.dram_tensor("out_x", (N, C), _mybir.dt.float32, kind="ExternalOutput").ap())
    build(nc, *args)
    return _run(nc, [arrays], core_ids=[0]).results[0]["out_x"]
```

```python
import concourse.bass as bass
from concourse import mybir
from contextlib import ExitStack

F32 = mybir.dt.float32
I32 = mybir.dt.int32
BF16 = mybir.dt.bfloat16
FP16 = mybir.dt.float16
U16 = mybir.dt.uint16
ALU = mybir.AluOpType
ACT = mybir.ActivationFunctionType
AX = mybir.AxisListType

P = 128
N = 3125
C = 256
HALF = C // 2
E = 53125
HEADS, D = 8, 64
HD = HEADS * D
T = -(-N // P)
LAST = N - (T - 1) * P
STEP = 12
COLS = -(-E // (P * STEP)) * STEP
FULL = E // COLS
TAIL = E - FULL * COLS
GP = 2
GROUPS = (E + T * (GP * P - 1)) // (GP * P)
CHUNKS = GROUPS * GP
QUAD = 4
QUADS = CHUNKS // QUAD
UNROLL = 4
SLOTS = UNROLL * QUAD
TILE_AT = 2
ROUNDS = CHUNKS // SLOTS
AHEAD = 2
SCATTERED = {"S": 18 * STEP, "D": COLS - (AHEAD + ROUNDS) * STEP}
PLACED = {o: COLS - SCATTERED[o] for o in "SD"}
STATS = 4
RING = 4
W1 = HD + HEADS
W2 = C + 1
PAD_CHUNKS = -(-COLS * (P - FULL) // (2 * P)) * 2
PITCH = CHUNKS + PAD_CHUNKS
REC = 4
BLOCK = 5
EPS = 1e-5
ALPHA = 0.2
assert CHUNKS % SLOTS == 0 and CHUNKS <= 512 and ROUNDS % 2 == 1 and RING * 4 == SLOTS and STEP % RING == 0
assert FULL < P and PITCH * REC % 8 == 0 and min(SCATTERED.values()) >= 2 * STEP
assert T % BLOCK == 0 and PLACED["S"] // STEP > 2 * (T // STATS)


def build(nc, x, src, dst, edge_weight, W_heads, b_heads, a_heads, g_heads, beta_heads,
          W_out, b_out, a_out, g_out, beta_out, out):
    ctx = ExitStack()
    with ctx:
        def sb(name, shape, dt=F32):
            return ctx.enter_context(nc.sbuf_tensor(name, shape, dt))

        def sem(name):
            return ctx.enter_context(nc.semaphore(name))

        ctx.enter_context(nc.allow_non_contiguous_dma(reason="small weight vectors"))
        bank = [ctx.enter_context(nc.psum_tensor(f"bank{i}", [P, 512], F32)) for i in range(8)]

        table_a = nc.dram_tensor("table_a", (T * P, HALF), F32, kind="Internal").ap()
        table_b = nc.dram_tensor("table_b", (T * P, HALF), F32, kind="Internal").ap()
        records = {o: nc.dram_tensor(f"records_{o}", (P * PITCH, REC), F32, kind="Internal").ap() for o in "SD"}
        table_1 = nc.dram_tensor("table_1", (T * P, W1), F32, kind="Internal").ap()
        table_2 = nc.dram_tensor("table_2", (T * P, W2), F32, kind="Internal").ap()

        iota_f = sb("iota_f", [P, 512])
        iota_lane = sb("iota_lane", [P, P], BF16)
        iota_chunk = sb("iota_chunk", [P, CHUNKS], FP16)
        row_i = sb("row_i", [P, 1], I32)
        row_f = sb("row_f", [P, 1])
        ident = sb("ident", [P, P])
        before = sb("before", [P, P])
        ones = sb("ones", [P, COLS])
        one_b = sb("one_b", [P, 1], BF16)
        eps = sb("eps", [P, 1])

        scratch = sb("scratch", [P, 12 * HD])

        def carve(at, a, b):
            return scratch[:, at:at + a * b].rearrange("p (a b) -> p a b", a=a)

        in_tile = scratch[:, 0:T * COLS // 2].bitcast(BF16).rearrange("p (t c) -> p t c", t=T)
        msg = carve(0, 2 * QUAD, HD)
        square = carve(0, 4, HD)
        neg_exp = carve(4 * HD, 2, HD)
        final = carve(6 * HD, 4, C)
        oh_count = scratch[:, 0:SLOTS * P // 2].bitcast(BF16).rearrange("p (a c) -> p a c", c=P)
        ohT = carve(8 * HD, 2, QUAD * P)
        featT = carve(10 * HD, 2, HD)
        off_by = carve(10 * HD, 2 * QUAD, P)
        scratch2 = sb("scratch2", [P, 7 * COLS])

        def row_of(n, width=COLS):
            return scratch2[:, n * COLS:n * COLS + width]

        lo_i, tile_f, pos, pos_i = row_of(0).bitcast(I32), row_of(1), row_of(2), row_of(3).bitcast(I32)
        rank = row_of(4, 2 * COLS).rearrange("p (a c) -> p a c", a=2)
        w_b = row_of(6, COLS // 2).bitcast(BF16)
        mask_now = row_of(6).bitcast(BF16).rearrange("p (a c) -> p a c", a=2)
        s_odd, s_node = row_of(2, CHUNKS), row_of(4, CHUNKS)
        iota_i = row_of(2, 512).bitcast(I32)
        stage = row_of(0, 2 * W1).rearrange("p (a c) -> p a c", a=2)

        at = 2 * W1
        head_mean = scratch2[:, at:at + T * HEADS].rearrange("p (t h) -> p t h", h=HEADS)
        head_var = scratch2[:, at + T * HEADS:at + 2 * T * HEADS].rearrange("p (t h) -> p t h", h=HEADS)

        xs = sb("xs", [P, T, C])
        work = sb("work", [P, T, HD])
        stats = sb("stats", [P, T, 6])
        mv = sb("mv", [P, T, 2])
        rstd = sb("rstd", [P, T])
        nbias = sb("nbias", [P, T])
        norm = work[:, :, 0:C]
        acc = {"S": work[:, :, C:C + HALF + 1], "D": work[:, :, 0:HALF + 1]}
        s_src1 = sb("s_src1", [P, T, HEADS])
        s_src2 = sb("s_src2", [P, T, 1])

        given = sb("given", [P, 15, COLS])
        nat = {"src": given[:, 0, :].bitcast(I32), "dst": given[:, 1, :].bitcast(I32)}
        nat_w = given[:, 2, :]
        key_lo = given[:, 3, :]
        w_part = given[:, 4:7, :]
        index = {"S": given[:, 7:9, :], "D": given[:, 11:13, :]}
        count = sb("count", [P, T])
        cap_i = sb("cap_i", [P, T], I32)
        cap = sb("cap", [P, T])
        cap_sum = sb("cap_sum", [P, T])
        first = sb("first", [P, T])
        chunk = {"S": given[:, 9, :], "D": given[:, 13, :]}
        lane = {"S": given[:, 10, :], "D": given[:, 14, :]}
        pad_at = sb("pad_at", [P, 1])
        group_no = sb("group_no", [P, 2])
        tile_of = sb("tile_of", [P, 2])
        group_tile = {o: sb(f"group_tile_{o}", [1, TILE_AT + GROUPS], I32) for o in "SD"}

        sort_ring = sb("sort_ring", [P, RING, CHUNKS + 6 * P], BF16)
        oh_chunk = sort_ring[:, :, 0:CHUNKS]
        oh_w = sort_ring[:, :, CHUNKS:CHUNKS + 3 * P].rearrange("p r (f c) -> p r f c", c=P)
        oh_i1 = sort_ring[:, :, CHUNKS + 3 * P:CHUNKS + 4 * P].bitcast(FP16)
        oh_i2 = sort_ring[:, :, CHUNKS + 4 * P:CHUNKS + 5 * P]
        oh_lane = sort_ring[:, :, CHUNKS + 5 * P:CHUNKS + 6 * P]
        by_pool = sb("by_pool", [P, CHUNKS, REC])
        s_lo = {"S": sb("s_lo_S", [P, CHUNKS])[:, :], "D": by_pool[:, :, 2]}
        s_idx = {"S": sb("s_idx_S", [P, CHUNKS], I32)[:, :], "D": by_pool[:, :, 3].bitcast(I32)}
        s_w = {"S": sb("s_w_S", [P, CHUNKS])[:, :], "D": by_pool[:, :, 0]}
        rdeg = sb("rdeg", [P, T, 1])

        idx_now = sb("idx_now", [P, 2, SLOTS], I32)
        rec_now = sb("rec_now", [P, 2, STEP, REC])
        rows_near = sb("rows_near", [P, SLOTS // 2, W1])
        rows_far = given[:, :, :].rearrange("p a c -> p (a c)")[:, 0:SLOTS // 2 * W1].rearrange("p (a c) -> p a c", c=W1)
        held = rows_near[:, :, :].rearrange("p a c -> p (a c)")
        rec, rec_row, at = {}, {}, SLOTS * HALF
        for o in "SD":
            n = SCATTERED[o]
            rec[o] = held[:, at:at + REC * n].rearrange("p (c f) -> p c f", f=REC)
            rec_row[o] = held[:, at + REC * n:at + (REC + 1) * n].bitcast(I32)
            at += (REC + 1) * n
        rows0 = rows_near[:, :, :].rearrange("p a c -> p (a c)")[:, 0:SLOTS * HALF].rearrange("p (a c) -> p a c", c=HALF)

        def row_slots(a, n):
            return (rows_near if a < SLOTS // 2 else rows_far)[:, a % (SLOTS // 2):a % (SLOTS // 2) + n, :]

        oh = sb("oh", [P, SLOTS, P])
        oh_flat = oh[:, :, :].rearrange("p a c -> p (a c)")
        wh = oh_flat[:, 0:4 * C].rearrange("p (k c) -> p k c", c=C)
        wo = oh_flat[:, 4 * C:4 * C + 2 * HD].rearrange("p (k c) -> p k c", c=HD)
        score = sb("score", [P, 2, QUAD * HEADS])
        lrelu = sb("lrelu", [P, 2, QUAD * HEADS])
        e_att = sb("e_att", [P, 2, QUAD * HEADS])

        gains = sort_ring[:, :, :].rearrange("p r c -> p (r c)")[:, 0:6 * (HD + C)].bitcast(F32)
        gh, betah = gains[:, 0:HD], gains[:, HD:2 * HD]
        go, betao = gains[:, 2 * HD:2 * HD + C], gains[:, 2 * HD + C:2 * (HD + C)]
        bias = {"1": gains[:, 2 * (HD + C):2 * (HD + C) + HD], "2": gains[:, 2 * (HD + C) + HD:3 * (HD + C)]}
        whT = sb("whT", [P, 2, HD])
        ah = sb("ah", [P, 4 * 2 * HEADS])
        ahT = sb("ahT", [P, 2, 2 * HEADS])
        bh_col = sb("bh_col", [P, 4])
        bah = sb("bah", [1, 2 * HEADS])
        woT = sb("woT", [P, 4, C + 2])
        ao = sb("ao", [P, 4])
        bo_col = sb("bo_col", [P, 2])
        bao = sb("bao", [1, 2])

        q_pad = sem("q_pad")
        pad_row = sem("pad_row")
        q_x = sem("q_x")
        q_edges = sem("q_edges")
        q_weights = sem("q_weights")
        q_gains = sem("q_gains")
        iota_made = sem("iota_made")
        consts_made = sem("consts_made")
        dve_chain = sem("dve_chain")
        act_chain = sem("act_chain")
        pe_chain = sem("pe_chain")
        w_evac = sem("w_evac")
        counted = sem("counted")
        tiles_found = sem("tiles_found")
        tiles_in_row = sem("tiles_in_row")
        offsets = sem("offsets")
        q_zero = sem("q_zero")
        acc_zeroed = sem("acc_zeroed")
        ranked = sem("ranked")
        rec_ready = sem("rec_ready")
        rec_staged = sem("rec_staged")
        scattered = {o: [sem(f"scattered_{o}{i}") for i in range(2)] for o in "SD"}
        q_by_pool = sem("q_by_pool")
        lane_ready = sem("lane_ready")
        fields_ready = sem("fields_ready")
        col_ready = sem("col_ready")
        col_free = sem("col_free")
        edges_sorted = sem("edges_sorted")
        stats_ready = sem("stats_ready")
        moments_ready = sem("moments_ready")
        std_ready = sem("std_ready")
        nb_ready = sem("nb_ready")
        normed = sem("normed")
        tab_ab = sem("tab_ab")
        tab_1 = [sem(f"tab_1{i}") for i in range(2)]
        tab_2 = [sem(f"tab_2{i}") for i in range(2)]
        gathered = [sem(f"gathered{i}") for i in range(SLOTS)]
        idx_ready = sem("idx_ready")
        chunks_summed = sem("chunks_summed")
        oh_ready = {o: sem(f"oh_ready_{o}") for o in "SD12"}
        sum_ready = {o: sem(f"sum_ready_{o}") for o in "12"}
        sum_free = {o: sem(f"sum_free_{o}") for o in "SD12"}
        ohT_psum = {o: sem(f"ohT_psum_{o}") for o in "12"}
        ohT_ready = {o: sem(f"ohT_ready_{o}") for o in "12"}
        ssrc_ready = {o: sem(f"ssrc_ready_{o}") for o in "12"}
        off_made = {o: sem(f"off_made_{o}") for o in "12"}
        z_ready = {o: sem(f"z_ready_{o}") for o in "12"}
        lrelu_ready = {o: sem(f"lrelu_ready_{o}") for o in "12"}
        e_ready = {o: sem(f"e_ready_{o}") for o in "12"}
        msg_ready = {o: sem(f"msg_ready_{o}") for o in "12"}
        featT_psum = {o: sem(f"featT_psum_{o}") for o in "12"}
        featT_ready = {o: sem(f"featT_ready_{o}") for o in "12"}
        dense_psum = {o: sem(f"dense_psum_{o}") for o in "12"}
        dense_dve = {o: sem(f"dense_dve_{o}") for o in "12"}
        acc_cleared = sem("acc_cleared")
        head_sum = sem("head_sum")
        centred = sem("centred")
        squared = sem("squared")
        square_used = sem("square_used")
        scaled = sem("scaled")
        gained = sem("gained")
        offset_added = sem("offset_added")
        exp_ready = sem("exp_ready")
        z_done = sem("z_done")
        final_ready = sem("final_ready")
        q_out = [sem(f"q_out{i}") for i in range(4)]

        def beside(k):
            return range(k * STEP // SLOTS, (k + 1) * STEP // SLOTS)

        def tile_numbers(engine, o, at, n):
            return nc.values_load_multi_w_load_instructions(
                group_tile[o][0:1, bass.ds(at, n)], engines=[engine], min_val=0, max_val=T - 1,
                skip_runtime_bounds_check_because="clamped to T - 1 when made")[1]

        block = ctx.enter_context(nc.Block())

        @block.sync
        def _(sp):
            sp.wait_ge(q_pad, 3)
            for k, d in (("src", src), ("dst", dst)):
                sp.dma_start(nat[k][0:FULL, :], d[0:FULL * COLS].rearrange("(p c) -> p c", c=COLS)).then_inc(q_edges, 16)
                sp.dma_start(nat[k][FULL:FULL + 1, 0:TAIL], d[FULL * COLS:E][None, :]).then_inc(q_edges, 16)
            sp.dma_start(nat_w[0:FULL, :], edge_weight[0:FULL * COLS].rearrange("(p c) -> p c", c=COLS)).then_inc(q_edges, 16)
            sp.dma_start(nat_w[FULL:FULL + 1, 0:TAIL], edge_weight[FULL * COLS:E][None, :]).then_inc(q_edges, 16)
            zeros = work[:, 0:8, C:C + PITCH * REC // 8]
            sp.wait_ge(acc_zeroed, 1)
            for o in "SD":
                sp.dma_start(records[o].rearrange("(p c) f -> p (c f)", p=P).rearrange("p (a b) -> p a b", a=8), zeros).then_inc(q_zero, 16)
            sp.wait_ge(pad_row, 1)
            sp.dma_start(xs[:, 0:T - 1, :], x[0:(T - 1) * P, :].rearrange("(t p) c -> p t c", p=P)).then_inc(q_x, 16)
            sp.dma_start(xs[0:LAST, T - 1, :], x[(T - 1) * P:N, :]).then_inc(q_x, 16)
            sp.dma_start(wh[:, :, :], W_heads.rearrange("(k q) d f -> (q d) k f", q=2)).then_inc(q_weights, 16)
            sp.wait_ge(q_pad, 4)
            for q in range(2):
                for s in range(2):
                    sp.dma_start(ah[D * q:D * q + D, q + HEADS * s:q + HEADS * s + 18 * 3 + 1:18],
                                 a_heads.rearrange("(k q) (s d) -> q s d k", q=2, s=2)[q, s]).then_inc(q_weights, 16)
            sp.dma_start(bh_col[:, :], b_heads.rearrange("(k q) d -> (q d) k", q=2)).then_inc(q_weights, 16)
            sp.dma_start(wo[:, :, :], W_out.rearrange("(k p) f -> p k f", p=P)).then_inc(q_weights, 16)
            sp.dma_start(ao[:, :], a_out.rearrange("(a p) -> p a", p=P)).then_inc(q_weights, 16)
            sp.dma_start(bo_col[:, :], b_out.rearrange("(k p) -> p k", p=P)).then_inc(q_weights, 16)

            sp.wait_ge(normed, T)
            for table, half in ((table_a, 0), (table_b, 1)):
                sp.dma_start(table.rearrange("(t p) c -> p t c", p=P),
                             work[:, :, half * HALF:(half + 1) * HALF]).then_inc(tab_ab, 16)

            def load_placed(o):
                for u in range(2):
                    sp.wait_ge(scattered[o][u], 16 * STEP * ((SCATTERED[o] // STEP + 1 - u) // 2))
                sp.dma_start(by_pool[:, :, :], records[o].rearrange("(p c) f -> p c f", p=P)[:, 0:CHUNKS, :]).then_inc(q_by_pool, 16)

            load_placed("S")
            sp.wait_ge(edges_sorted, 1)
            load_placed("D")
            sp.wait_ge(edges_sorted, 2)
            sp.dma_start(bias["1"], b_heads.rearrange("h d -> (h d)").partition_broadcast(P)).then_inc(q_gains, 16)
            sp.dma_start(bias["2"], b_out.partition_broadcast(P)).then_inc(q_gains, 16)
            sp.dma_start(gh[:, :], g_heads.rearrange("h d -> (h d)").partition_broadcast(P)).then_inc(q_gains, 16)
            sp.dma_start(betah[:, :], beta_heads.rearrange("h d -> (h d)").partition_broadcast(P)).then_inc(q_gains, 16)
            sp.dma_start(go[:, :], g_out.partition_broadcast(P)).then_inc(q_gains, 16)
            sp.dma_start(betao[:, :], beta_out.partition_broadcast(P)).then_inc(q_gains, 16)

            for o, table, width, landed in (("1", table_1, W1, tab_1), ("2", table_2, W2, tab_2)):
                for t in range(T):
                    sp.wait_ge(dense_dve[o], t + 1)
                    sp.dma_start(table[t * P:(t + 1) * P, :], stage[:, t % 2, 0:width]).then_inc(landed[t % 2], 16)

            for t in range(T):
                n = P if t < T - 1 else LAST
                sp.wait_ge(final_ready, t + 1)
                sp.dma_start(out[t * P:t * P + n, :], final[0:n, t % 4, :]).then_inc(q_out[t % 4], 16)
            for k in range(4):
                sp.wait_ge(q_out[k], 16 * ((T + 3 - k) // 4))

        @block.gpsimd
        def _(pool):
            nc.gpsimd.iota(iota_i[:, :], pattern=[[1, 512]], base=0, channel_multiplier=0).then_inc(iota_made, 1)
            nc.gpsimd.iota(row_i[:, :], pattern=[[0, 1]], base=0, channel_multiplier=1).then_inc(iota_made, 1)
            nc.gpsimd.memset(xs[:, T - 1, :], 0.0).then_inc(pad_row, 1)
            nc.gpsimd.memset(work[:, :, C:HD], 0.0).then_inc(acc_zeroed, 1)

            def round_indices(phase, order, r, u):
                nc.gpsimd.tensor_copy(idx_now[:, u, :], s_idx[order][:, bass.ds(r * SLOTS, SLOTS)]).then_inc(idx_ready, 1)
                pool.wait_ge(idx_ready, r + (phase * ROUNDS + 1))

            def gather(table, to, u, b):
                nc.gpsimd.indirect_dma_start(
                    out=to, out_offset=None, in_=table[:, :],
                    in_offset=bass.IndirectOffsetOnAxis(ap=idx_now[:, u, b:b + 1], axis=0),
                ).then_inc(gathered[b], 16)

            def gather_layer0(phase, order, table):
                def turn(r, u):
                    round_indices(phase, order, r, u)
                    for b in range(SLOTS):
                        pool.wait_ge(chunks_summed, r * SLOTS + (phase * CHUNKS + b + 1))
                        pool.nop(nofuse=True)
                        gather(table, rows0[:, b, :], u, b)

                turn(0, phase % 2)
                with pool.Fori(0, ROUNDS // 2) as i:
                    for u in range(2):
                        turn(i * 2 + (u + 1), (phase + u + 1) % 2)

            def gather_layer1(o, table, width):
                phase = 1 + int(o)

                def to(b):
                    return row_slots(b, 1)[:, 0, 0:width]

                round_indices(phase, "S", 0, phase % 2)
                for b in range(SLOTS):
                    gather(table, to(b), phase % 2, b)
                with pool.Fori(0, ROUNDS // 2) as i:
                    for u in range(2):
                        r, side = i * 2 + (u + 1), (phase + u + 1) % 2
                        round_indices(phase, "S", r, side)
                        for b in range(SLOTS):
                            pool.wait_ge(msg_ready[o], r * SLOTS + (b + 1 - SLOTS))
                            pool.nop(nofuse=True)
                            gather(table, to(b), side, b)

            pool.wait_ge(q_zero, 32)

            def scatter(o, r, u, first, before):
                if not first:
                    pool.wait_ge(scattered[o][u], (r - u) * (8 * STEP))
                nc.gpsimd.tensor_copy(rec_now[:, u, :, :].rearrange("p c f -> p (c f)"),
                                      rec[o][:, bass.ds(r * STEP, STEP), :].rearrange("p c f -> p (c f)")).then_inc(rec_staged, 1)
                nc.gpsimd.tensor_copy(idx_now[:, u, 0:STEP], rec_row[o][:, bass.ds(r * STEP, STEP)]).then_inc(rec_staged, 1)
                pool.wait_ge(rec_staged, r * 2 + (before * 2 + 2))
                pool.nop(nofuse=True)
                for b in range(STEP):
                    nc.gpsimd.indirect_dma_start(
                        out=records[o][:, :], out_offset=bass.IndirectOffsetOnAxis(ap=idx_now[:, u, b:b + 1], axis=0),
                        in_=rec_now[:, u, b, :], in_offset=None).then_inc(scattered[o][u], 16)

            def scatter_all(o, before):
                turns = SCATTERED[o] // STEP
                for u in range(2):
                    scatter(o, u, u, True, before)
                if turns >= 4:
                    with pool.Fori(1, turns // 2) as i:
                        for u in range(2):
                            scatter(o, i * 2 + u, u, False, before)
                if turns % 2:
                    scatter(o, turns - 1, 0, False, before)
                for u in range(2):
                    pool.wait_ge(scattered[o][u], 16 * STEP * ((turns + 1 - u) // 2))

            pool.wait_ge(rec_ready, 1)
            scatter_all("S", 0)
            pool.wait_ge(rec_ready, 2)
            scatter_all("D", SCATTERED["S"] // STEP)
            pool.wait_ge(edges_sorted, 1)
            pool.wait_ge(tab_ab, 32)
            gather_layer0(0, "S", table_a)
            nc.gpsimd.memset(acc["D"], 0.0).then_inc(acc_zeroed, 1)
            pool.wait_ge(edges_sorted, 2)
            gather_layer0(1, "D", table_b)

            def clear(o, t, width):
                pool.wait_ge(featT_psum[o], t + 1)
                nc.gpsimd.memset(work[:, t, 0:width], 0.0).then_inc(acc_cleared, 1)

            for t in range(T):
                clear("1", t, HD)
            pool.wait_ge(tab_1[0], 16 * ((T + 1) // 2))
            pool.wait_ge(tab_1[1], 16 * (T // 2))
            gather_layer1("1", table_1, W1)

            pool.wait_ge(q_gains, 16 * 6)
            for t in range(T):
                pool.wait_ge(head_sum, t + 1)
                y = work[:, t, :].rearrange("p (h d) -> p h d", h=HEADS)
                nc.gpsimd.tensor_tensor(y, y, head_mean[:, t, :].unsqueeze(2).to_broadcast([P, HEADS, D]), ALU.subtract).then_inc(centred, 1)

            LAG = 4
            for t in range(T + LAG):
                if t < T:
                    pool.wait_ge(scaled, t + 1)
                    nc.gpsimd.tensor_tensor(work[:, t, :], work[:, t, :], gh[:, :], ALU.mult).then_inc(gained, 1)
                if t >= LAG:
                    clear("2", t - LAG, C)
            pool.wait_ge(tab_2[0], 16 * ((T + 1) // 2))
            pool.wait_ge(tab_2[1], 16 * (T // 2))
            gather_layer1("2", table_2, W2)
            for t in range(T):
                pool.wait_ge(scaled, T + t + 1)
                nc.gpsimd.tensor_tensor(work[:, t, 0:C], work[:, t, 0:C], betao[:, :], ALU.add).then_inc(offset_added, 1)

        @block.scalar
        def _(act):
            def sort_fields(o, i, before, between=None):
                for k in range(STEP):
                    c, slot = i * STEP + k, k % RING
                    if between and k * STATS % STEP == 0:
                        between(k * STATS // STEP)
                    act.wait_ge(lane_ready, i * STEP + (before + k + 1))
                    for f in range(0 if o == "D" else 1, 3):
                        nc.scalar.activation(oh_w[:, slot, f, :], oh_lane[:, slot, :], ACT.Copy, scale=w_part[:, f, bass.ds(c, 1)])
                    nc.scalar.activation(oh_i2[:, slot, :], oh_lane[:, slot, :], ACT.Copy,
                                         scale=index[o][:, 1, bass.ds(c, 1)]).then_inc(fields_ready, 1)

            def normalise(t):
                nc.scalar.activation(norm[:, bass.ds(t, 1), :].rearrange("p t c -> p (t c)"), xs[:, bass.ds(t, 1), :].rearrange("p t c -> p (t c)"),
                                     ACT.Relu, bias=nbias[:, bass.ds(t, 1)], scale=rstd[:, bass.ds(t, 1)]).then_inc(normed, 1)

            half = T // STATS
            with act.Fori(0, half) as i:
                sort_fields("S", i, 0)
            act.wait_ge(moments_ready, T)
            nc.scalar.activation(rstd[:, :], mv[:, :, 1], ACT.Sqrt, bias=eps[:, :]).then_inc(std_ready, 1)
            act.wait_ge(nb_ready, 1)
            with act.Fori(half, 2 * half) as i:
                sort_fields("S", i, 0, lambda u: normalise(i * STATS + (u - STATS * half)))
            for t in range(STATS * half, T):
                normalise(t)
            with act.Fori(2 * half, PLACED["S"] // STEP) as i:
                sort_fields("S", i, 0)
            with act.Fori(0, AHEAD + ROUNDS) as i:
                sort_fields("D", i, PLACED["S"])

            def evacuate_features(o, t, nk):
                act.wait_ge(featT_psum[o], t + 1)
                if t >= 2:
                    act.wait_ge(dense_psum[o], t - 1)
                nc.scalar.copy(featT[:, t % 2, 0:nk], bank[t % 2][:, 0:nk]).then_inc(featT_ready[o], 1)

            for b in range(1, T // BLOCK + 2):
                if b <= T // BLOCK:
                    act.wait_ge(moments_ready, T + b * BLOCK)
                    nc.scalar.activation(rstd[:, (b - 1) * BLOCK:b * BLOCK], mv[:, (b - 1) * BLOCK:b * BLOCK, 1], ACT.Sqrt,
                                         bias=eps[:, :]).then_inc(std_ready, 1)
                    act.wait_ge(nb_ready, 1 + b)
                for t in range((b - 1) * BLOCK, b * BLOCK):
                    if b <= T // BLOCK:
                        normalise(t)
                    if b >= 2:
                        evacuate_features("1", t - BLOCK, C)

            def attend(o):
                heads = HEADS if o == "1" else 1

                def one_hots(q, u):
                    side = u % 2 * QUAD
                    if not isinstance(q, int) or q >= 2:
                        act.wait_ge(oh_ready[o], q - 1)
                    for k in range(QUAD):
                        last = nc.scalar.activation(off_by[:, side + k, :], iota_f[:, 0:P], ACT.Abs, scale=-1.0,
                                                    bias=s_lo["S"][:, bass.ds(q * QUAD + k, 1)])
                    last.then_inc(off_made[o], 1)
                    act.wait_ge(off_made[o], q + 1)
                    nc.scalar.activation(oh[:, u % UNROLL * QUAD:(u % UNROLL + 1) * QUAD, :], off_by[:, side:side + QUAD, :], ACT.Relu,
                                         scale=-1.0, bias=ones[:, 0:1]).then_inc(oh_ready[o], 1)

                def transposed(q, u):
                    act.wait_ge(ohT_psum[o], q + 1)
                    nc.scalar.activation(ohT[:, u % 2, :], bank[u % 2][:, :], ACT.Copy).then_inc(ohT_ready[o], 1)

                def weights(q, u):
                    act.wait_ge(lrelu_ready[o], q + 1)
                    nc.scalar.activation(e_att[:, u % 2, 0:QUAD * heads], lrelu[:, u % 2, 0:QUAD * heads], ACT.Exp,
                                         scale=-1.0).then_inc(e_ready[o], 1)

                def turn(i):
                    for u in range(UNROLL):
                        q = i * UNROLL + u
                        if not isinstance(i, int) or q + 1 < QUADS:
                            weights(i * UNROLL + (u + 1), u + 1)
                        if not isinstance(i, int) or q + 2 < QUADS:
                            transposed(i * UNROLL + (u + 2), u)
                        if not isinstance(i, int) or q + 3 < QUADS:
                            if not isinstance(i, int) or q >= 1:
                                act.wait_ge(sum_ready[o], i * (2 * UNROLL) + 2 * u)
                            one_hots(i * UNROLL + (u + 3), u + 3)

                act.wait_ge(dense_psum[o], T)
                for q in range(3):
                    one_hots(q, q)
                transposed(0, 0)
                transposed(1, 1)
                weights(0, 0)
                turn(0)
                with act.Fori(1, ROUNDS - 1) as i:
                    turn(i)
                turn(ROUNDS - 1)

            def elu_exponential(n, slot, y):
                e = neg_exp[:, slot, 0:y.shape[-1]]
                act.wait_ge(offset_added, n + 1)
                if n >= 2:
                    act.wait_ge(z_done, n - 1)
                nc.scalar.activation(e, y, ACT.Relu, scale=-1.0).then_inc(act_chain, 1)
                act.wait_ge(act_chain, n + 1)
                nc.scalar.activation(e, e, ACT.Exp, scale=-1.0).then_inc(exp_ready, 1)

            attend("1")
            for t in range(T):
                act.wait_ge(centred, t + 1)
                if t >= 4:
                    act.wait_ge(square_used, t - 3)
                nc.scalar.activation(square[:, t % 4, :], work[:, t, :], ACT.Square).then_inc(squared, 1)
            act.wait_ge(square_used, T)
            nc.scalar.activation(head_var[:, :, :], head_var[:, :, :], ACT.Sqrt, bias=eps[:, :], scale=1.0 / D).then_inc(std_ready, 1)
            for t in range(T + 2):
                if t < T:
                    elu_exponential(t, t % 2, work[:, t, :])
                if t >= 2:
                    evacuate_features("2", t - 2, HD)
            attend("2")
            act.wait_ge(moments_ready, 3 * T)
            nc.scalar.activation(rstd[:, :], mv[:, :, 1], ACT.Sqrt, bias=eps[:, :]).then_inc(std_ready, 1)
            act.wait_ge(nb_ready, 2 + T // BLOCK)
            for t in range(T + 2):
                if t < T:
                    act.wait_ge(gained, T + t + 1)
                    nc.scalar.activation(work[:, t, 0:C], work[:, t, 0:C], ACT.Copy, scale=rstd[:, t:t + 1]).then_inc(scaled, 1)
                if t >= 2:
                    elu_exponential(T + t - 2, (T + t) % 2, work[:, t - 2, 0:C])

        @block.tensor
        def _(pe):
            def prefix(n):
                pe.wait_ge(counted, T * (n + 1))
                nc.tensor.matmul(bank[6][:, 0:T], before[:, :], count[:, :], start=True, stop=True)
                nc.tensor.matmul(bank[7][:, 0:T], ones[:, 0:P], count[:, :], start=True, stop=True).then_inc(offsets, 1)
                pe.wait_ge(tiles_found, n + 1)
                for j in range(2):
                    last = nc.tensor.matmul(bank[7][0:1, (2 + j) * P:(3 + j) * P], tile_of[:, j:j + 1], ident[:, :],
                                            start=True, stop=True)
                last.then_inc(tiles_in_row, 1)

            pe.wait_ge(consts_made, 1)
            prefix(0)
            pe.wait_ge(q_weights, 16 * 9)
            for k in range(4):
                for m in range(2):
                    nc.tensor.transpose(bank[m][:, k * P:(k + 1) * P], wh[:, k, m * P:(m + 1) * P], ident[:, :])
            for k in range(2):
                for m in range(4):
                    b = bank[2 + m // 2][:, (m % 2) * C + k * P:(m % 2) * C + (k + 1) * P]
                    nc.tensor.transpose(b, wo[:, k, m * P:(m + 1) * P], ident[:, :])
            for m in range(2):
                for k in range(4):
                    nc.tensor.matmul(bank[4][:, m * 16:m * 16 + 16], wh[:, k, m * P:(m + 1) * P],
                                     ah[:, k * 16:(k + 1) * 16], start=(k == 0), stop=(k == 3))
            for m in range(4):
                for k in range(2):
                    nc.tensor.matmul(bank[4][:, 32 + 2 * m:34 + 2 * m], wo[:, k, m * P:(m + 1) * P],
                                     ao[:, k:k + 3:2], start=(k == 0), stop=(k == 1))
            for k in range(4):
                nc.tensor.matmul(bank[5][0:1, 0:16], bh_col[:, k:k + 1], ah[:, k * 16:(k + 1) * 16],
                                 start=(k == 0), stop=(k == 3))
            for k in range(2):
                last = nc.tensor.matmul(bank[5][0:1, 16:18], bo_col[:, k:k + 1], ao[:, k:k + 3:2],
                                        start=(k == 0), stop=(k == 1))
            last.then_inc(pe_chain, 1)

            def sort_place(c, slot, start, stop):
                pe.wait_ge(col_ready, c)
                pe.wait_ge(fields_ready, c)
                for f in range(3):
                    nc.tensor.matmul(bank[0][:, 0:CHUNKS], oh_w[:, slot, f, :], oh_chunk[:, slot, :],
                                     start=start and f == 0, stop=stop and f == 2)
                nc.tensor.matmul(bank[1][:, 0:CHUNKS], oh_i1[:, slot, :], oh_chunk[:, slot, :], start=start, stop=stop)
                nc.tensor.matmul(bank[2][:, 0:CHUNKS], oh_i2[:, slot, :], oh_chunk[:, slot, :], start=start, stop=stop).then_inc(col_free, 1)

            def sort_turn(i, columns, before, at_start=False, at_end=False):
                for k in columns:
                    sort_place(i * STEP + (before + k + 1), k % RING, at_start and k == 0, at_end and k == STEP - 1)

            def sum_rows(o, phase, i, k):
                c = i * SLOTS + k
                g = i * (SLOTS // GP) + k // GP
                if k % GP == 0:
                    pe.wait_ge(sum_free[o], g + 1)
                pe.wait_ge(oh_ready[o], c + 1)
                pe.wait_ge(gathered[k], i * 16 + 16 * (phase * ROUNDS + 1))
                b = bank[4 + (k // GP) % 4]
                nc.tensor.matmul(b[:, 0:HALF], oh[:, k, :], rows0[:, k, :], start=(k % GP == 0), stop=False)
                nc.tensor.matmul(b[:, HALF:HALF + 1], oh_count[:, k, :], one_b[:, :], start=False,
                                 stop=(k % GP == GP - 1)).then_inc(chunks_summed, 1)

            pe.wait_ge(w_evac, 1)
            turns = PLACED["S"] // STEP
            sort_turn(0, range(STEP), 0, at_start=True)
            with pe.Fori(1, T // STATS) as i:
                sort_turn(i, range(STEP), 0)
            prefix(1)
            with pe.Fori(T // STATS, turns - 1) as i:
                sort_turn(i, range(STEP), 0)
            sort_turn(turns - 1, range(STEP), 0, at_end=True)

            def round_and_sort(i, at_end=False):
                for k in range(SLOTS):
                    sort_turn(i, beside(k), PLACED["S"] + AHEAD * STEP, at_end=at_end)
                    sum_rows("S", 0, i, k)

            for t in range(AHEAD):
                sort_turn(t, range(STEP), PLACED["S"], at_start=(t == 0))
            with pe.Fori(0, ROUNDS - 1) as i:
                round_and_sort(i)
            round_and_sort(ROUNDS - 1, at_end=True)
            with pe.Fori(0, ROUNDS) as i:
                for k in range(SLOTS):
                    sum_rows("D", 1, i, k)

            def dense(o, nk, width, rhs, rhs_s, b_s, ns, feats_ready, feat):
                for t in range(T + 1):
                    if t < T:
                        feats_ready(t)
                        if t >= 2:
                            pe.wait_ge(featT_ready[o], t - 1)
                        for k in range(nk):
                            last = nc.tensor.transpose(bank[t % 2][:, k * P:(k + 1) * P], feat[:, t, k * P:(k + 1) * P], ident[:, :])
                        last.then_inc(featT_psum[o], 1)
                    if t >= 1:
                        u = t - 1
                        pe.wait_ge(featT_ready[o], u + 1)
                        if u >= 2:
                            pe.wait_ge(dense_dve[o], u - 1)
                        for k in range(nk):
                            last = nc.tensor.matmul(bank[2 + u % 2][:, 0:width], featT[:, u % 2, k * P:(k + 1) * P], rhs[:, k, :],
                                                    start=(k == 0), stop=(k == nk - 1 and rhs_s is not None))
                        if rhs_s is None:
                            last = nc.tensor.matmul(bank[2 + u % 2][:, width - ns:width], ones[0:1, 0:P], b_s[0:1, :], start=False, stop=True)
                        else:
                            nc.tensor.matmul(bank[4 + u % 2][:, 0:ns], ones[0:1, 0:P], b_s[0:1, :], start=True, stop=False)
                            for k in range(nk):
                                last = nc.tensor.matmul(bank[4 + u % 2][:, 0:ns], featT[:, u % 2, k * P:(k + 1) * P], rhs_s[:, k, :],
                                                        start=False, stop=(k == nk - 1))
                        last.then_inc(dense_psum[o], 1)

            def attend(o):
                heads, width, s_src = (HEADS, HD, s_src1) if o == "1" else (1, C, s_src2)

                def transposed(q, u):
                    pe.wait_ge(oh_ready[o], q + 1)
                    for k in range(QUAD):
                        last = nc.tensor.transpose(bank[u % 2][:, k * P:(k + 1) * P], oh[:, u % UNROLL * QUAD + k, :], ident[:, :])
                    last.then_inc(ohT_psum[o], 1)

                def source_scores(q, u, tiles):
                    pe.wait_ge(ohT_ready[o], q + 1)
                    for k in range(QUAD):
                        last = nc.tensor.matmul(bank[2 + u % 2][:, k * heads:(k + 1) * heads], ohT[:, u % 2, k * P:(k + 1) * P],
                                                s_src[:, bass.ds(tiles[k // 2], 1), :].rearrange("p t h -> p (t h)"),
                                                start=True, stop=True)
                    last.then_inc(ssrc_ready[o], 1)

                def sums(q, u):
                    for k in range(QUAD):
                        if k % GP == 0:
                            pe.wait_ge(sum_free[o], q * 2 + (k // GP + 1))
                        pe.wait_ge(msg_ready[o], q * QUAD + (k + 1))
                        mm = nc.tensor.matmul(bank[4 + u % 2 * 2 + k // GP][:, 0:width], oh[:, u * QUAD + k, :],
                                              msg[:, u % 2 * QUAD + k, 0:width], start=(k % GP == 0), stop=(k % GP == GP - 1))
                        if k % GP == GP - 1:
                            mm.then_inc(sum_ready[o], 1)

                def turn(i):
                    n = 2 * UNROLL if not isinstance(i, int) or i < ROUNDS - 1 else 2 * UNROLL - 2
                    tiles = tile_numbers(mybir.EngineType.PE, "S", i * (2 * UNROLL) + (TILE_AT + 2), n)
                    for u in range(UNROLL):
                        q = i * UNROLL + u
                        if not isinstance(i, int) or q + 1 < QUADS:
                            source_scores(i * UNROLL + (u + 1), u + 1, tiles[2 * u:2 * u + 2])
                        if not isinstance(i, int) or q + 2 < QUADS:
                            transposed(i * UNROLL + (u + 2), u + 2)
                        sums(q, u)

                transposed(0, 0)
                transposed(1, 1)
                source_scores(0, 0, tile_numbers(mybir.EngineType.PE, "S", TILE_AT, 2))
                turn(0)
                with pe.Fori(1, ROUNDS - 1) as i:
                    turn(i)
                turn(ROUNDS - 1)

            dense("1", 2, HD, whT, ahT, bah, 2 * HEADS, lambda t: pe.wait_ge(normed, T + t + 1), norm)
            pe.wait_ge(dense_dve["1"], T)
            attend("1")
            dense("2", 4, C + 2, woT, None, bao, 2, lambda t: pe.wait_ge(z_done, t + 1), work)
            pe.wait_ge(dense_dve["2"], T)
            attend("2")

        @block.vector
        def _(dve):
            v = nc.vector
            linked = [0]

            def link(ins):
                linked[0] += 1
                ins.then_inc(dve_chain, 1)
                dve.wait_ge(dve_chain, linked[0])

            v.memset(nat["src"][:, :], T * P).then_inc(q_pad, 1)
            v.memset(nat["dst"][:, :], T * P).then_inc(q_pad, 1)
            v.memset(nat_w[:, :], 0.0).then_inc(q_pad, 1)
            v.memset(ah[:, :], 0.0).then_inc(q_pad, 1)
            v.memset(ones[:, :], 1.0)
            v.memset(eps[:, :], EPS)
            v.memset(one_b[:, :], 1.0)
            for o in "SD":
                v.memset(group_tile[o][0:1, 0:TILE_AT], 0)
            dve.wait_ge(iota_made, 2)
            link(v.tensor_copy(iota_f[:, :], iota_i[:, :]))
            link(v.tensor_copy(row_f[:, :], row_i[:, :]))
            link(v.tensor_scalar(pad_at[:, :], row_f[:, :], float(-FULL), 0.0, ALU.add, ALU.max))
            link(v.tensor_scalar(pad_at[:, :], pad_at[:, :], float(COLS), float(P * CHUNKS + 1), ALU.mult, ALU.add))
            v.tensor_copy(group_no[:, 0:1], row_f[:, :])
            v.tensor_scalar(group_no[:, 1:2], row_f[:, :], float(P), None, ALU.add)
            v.tensor_copy(iota_lane[:, :], iota_i[:, 0:P])
            v.tensor_copy(iota_chunk[:, :], iota_i[:, 0:CHUNKS])
            v.tensor_scalar(ident[:, :], iota_f[:, 0:P], row_f[:, :], None, ALU.is_equal)
            link(v.tensor_scalar(before[:, :], iota_f[:, 0:P], row_f[:, :], None, ALU.is_gt))
            dve.sem_inc(consts_made, 1)
            dve.sem_inc(chunks_summed, SLOTS)
            dve.sem_inc(col_free, RING)
            for o in "SD":
                dve.sem_inc(sum_free[o], 4)

            def tile_statistics(t):
                v.bn_stats(stats[:, bass.ds(t, 1), :].rearrange("p t c -> p (t c)"),
                           xs[:, bass.ds(t, 1), :].rearrange("p t c -> p (t c)")).then_inc(stats_ready, 1)

            def tile_moments(t, before):
                dve.wait_ge(stats_ready, t + (before + 1))
                v.bn_aggr(mv[:, t, :], stats[:, t, :]).then_inc(moments_ready, 1)

            def scales(n, a, b):
                dve.wait_ge(std_ready, n + 1)
                link(v.reciprocal(rstd[:, a:b], rstd[:, a:b]))
                v.scalar_tensor_tensor(out=nbias[:, a:b], in0=mv[:, a:b, 0], scalar=-1.0, in1=rstd[:, a:b],
                                       op0=ALU.mult, op1=ALU.mult).then_inc(nb_ready, 1)

            def at_t(a, t):
                return a[:, bass.ds(t, 1), :].rearrange("p t c -> p (t c)")

            def split_key(key):
                link(v.tensor_scalar(lo_i[:, :], key, P - 1, None, ALU.bitwise_and))
                link(v.tensor_copy(key_lo[:, :], lo_i[:, :]))
                link(v.tensor_scalar(lo_i[:, :], key, 7, None, ALU.logical_shift_right))
                link(v.tensor_copy(tile_f[:, :], lo_i[:, :]))

            def count_tile(t):
                v.tensor_scalar(at_t(in_tile, t), tile_f[:, :], iota_f[:, bass.ds(t, 1)], 0.0, ALU.is_equal, ALU.add,
                                accum_out=count[:, bass.ds(t, 1)]).then_inc(counted, 1)

            def rank_tile(t, side, before):
                mask = at_t(in_tile, t)
                if not isinstance(t, int):
                    v.tensor_copy(mask_now[:, side, :], mask)
                    mask = mask_now[:, side, :]
                v.tensor_tensor_scan(rank[:, side, :], ones[:, :], at_t(in_tile, t), first[:, bass.ds(t, 1)],
                                     ALU.mult, ALU.add).then_inc(ranked, 1)
                dve.wait_ge(ranked, t + (before + 1))
                if not isinstance(t, int):
                    dve.nop(nofuse=True)
                return v.copy_predicated(pos[:, :], mask.bitcast(U16), rank[:, side, :])

            def first_positions(n):
                dve.wait_ge(offsets, n + 1)
                link(v.tensor_scalar(cap[:, :], bank[7][:, 0:T], float(GP * P - 1), None, ALU.add))
                link(v.tensor_copy(cap_i[:, :], cap[:, :]))
                link(v.tensor_scalar(cap_i[:, :], cap_i[:, :], 8, None, ALU.logical_shift_right))
                link(v.tensor_copy(cap[:, :], cap_i[:, :]))
                link(v.tensor_tensor_scan(cap_sum[:, :], ones[:, 0:T], cap[:, :], 0.0, ALU.mult, ALU.add))
                link(v.tensor_sub(first[:, :], cap_sum[:, :], cap[:, :]))
                link(v.scalar_tensor_tensor(out=first[:, :], in0=first[:, :], scalar=float(GP * P), in1=bank[6][:, 0:T],
                                            op0=ALU.mult, op1=ALU.add))
                for j in range(2):
                    last = v.tensor_scalar(pos[:, 0:T], cap_sum[:, :], group_no[:, j:j + 1], 0.0, ALU.is_le, ALU.add,
                                           accum_out=tile_of[:, j:j + 1])
                    link(last)
                v.tensor_scalar(tile_of[:, :], tile_of[:, :], float(T - 1), None, ALU.min).then_inc(tiles_found, 1)
                link(v.tensor_scalar(pos[:, :], iota_f[:, 0:COLS], pad_at[:, :], None, ALU.add))

            def chunks_and_lanes(o, n, last):
                link(last)
                link(v.tensor_scalar(pos[:, :], pos[:, :], -1.0, None, ALU.add))
                link(v.tensor_copy(pos_i[:, :], pos[:, :]))
                link(v.tensor_scalar(lo_i[:, :], pos_i[:, :], P - 1, None, ALU.bitwise_and))
                link(v.tensor_copy(lane[o], lo_i[:, :]))
                link(v.tensor_scalar(lo_i[:, :], pos_i[:, :], 7, None, ALU.logical_shift_right))
                link(v.tensor_copy(chunk[o], lo_i[:, :]))
                dve.wait_ge(tiles_in_row, n + 1)
                v.tensor_copy(group_tile[o][0:1, TILE_AT:], bank[7][0:1, 2 * P:2 * P + GROUPS])

            def make_records(o, other):
                at = PLACED[o]
                v.tensor_copy(rec[o][:, :, 0], nat_w[:, at:COLS])
                v.tensor_copy(rec[o][:, :, 1], other[:, at:COLS])
                v.tensor_scalar(rec[o][:, :, 2], key_lo[:, at:COLS], 1.0, None, ALU.add)
                v.memset(rec[o][:, :, 3], 0.0)
                link(v.scalar_tensor_tensor(out=pos[:, at:COLS], in0=lane[o][:, at:COLS], scalar=float(PITCH), in1=chunk[o][:, at:COLS],
                                            op0=ALU.mult, op1=ALU.add))
                v.tensor_copy(rec_row[o], pos[:, at:COLS]).then_inc(rec_ready, 1)

            def weight_parts():
                link(v.tensor_copy(w_b[:, :], nat_w[:, :]))
                link(v.tensor_copy(w_part[:, 0, :], w_b[:, :]))
                link(v.tensor_sub(tile_f[:, :], nat_w[:, :], w_part[:, 0, :]))
                link(v.tensor_copy(w_b[:, :], tile_f[:, :]))
                link(v.tensor_copy(w_part[:, 1, :], w_b[:, :]))
                link(v.tensor_sub(w_part[:, 2, :], tile_f[:, :], w_part[:, 1, :]))

            def index_fields(o, other):
                link(v.tensor_scalar(lo_i[:, :], other, 1, None, ALU.logical_shift_right))
                link(v.tensor_copy(index[o][:, 0, :], lo_i[:, :]))
                link(v.tensor_scalar(lo_i[:, :], other, 1, None, ALU.bitwise_and))
                link(v.tensor_copy(index[o][:, 1, :], lo_i[:, :]))
                link(v.scalar_tensor_tensor(out=index[o][:, 1, :], in0=index[o][:, 1, :], scalar=float(P), in1=key_lo,
                                            op0=ALU.mult, op1=ALU.add))
                link(v.tensor_scalar(index[o][:, 1, :], index[o][:, 1, :], 1.0, None, ALU.add))

            def sort_column(o, c, slot, before):
                dve.wait_ge(col_free, c + (before + 1))
                at = lane[o][:, bass.ds(c, 1)]
                v.tensor_scalar(oh_lane[:, slot, :], iota_lane[:, :], at, None, ALU.is_equal).then_inc(lane_ready, 1)
                v.tensor_scalar(oh_chunk[:, slot, :], iota_chunk[:, :], chunk[o][:, bass.ds(c, 1)], None, ALU.is_equal)
                if o == "S":
                    v.tensor_scalar(oh_w[:, slot, 0, :], iota_lane[:, :], at, w_part[:, 0, bass.ds(c, 1)], ALU.is_equal, ALU.mult)
                v.tensor_scalar(oh_i1[:, slot, :], iota_lane[:, :], at, index[o][:, 0, bass.ds(c, 1)], ALU.is_equal,
                                ALU.mult).then_inc(col_ready, 1)

            def merge(o, n, columns):
                dve.wait_ge(col_free, RING + columns)
                dve.wait_ge(q_by_pool, 16 * (n + 1))
                link(v.tensor_scalar(s_node[:, :], bank[2][:, 0:CHUNKS], -1.0, None, ALU.add))
                link(v.tensor_scalar(s_odd[:, :], s_node[:, :], float(P), None, ALU.is_ge))
                link(v.scalar_tensor_tensor(out=s_node[:, :], in0=s_odd[:, :], scalar=-float(P), in1=s_node[:, :],
                                            op0=ALU.mult, op1=ALU.add))
                link(v.tensor_tensor(s_lo[o], s_node[:, :], by_pool[:, :, 2], ALU.add))
                link(v.scalar_tensor_tensor(out=s_node[:, :], in0=bank[1][:, 0:CHUNKS], scalar=2.0, in1=s_odd[:, :],
                                            op0=ALU.mult, op1=ALU.add))
                v.tensor_tensor(s_idx[o], s_node[:, :], by_pool[:, :, 1], ALU.add)
                link(v.tensor_tensor(s_w[o], bank[0][:, 0:CHUNKS], by_pool[:, :, 0], ALU.add))
                dve.sem_inc(edges_sorted, 1)

            def weighted_one_hot(o, phase, i, k):
                c = i * SLOTS + k
                dve.wait_ge(chunks_summed, c + (phase * CHUNKS + 1))
                v.tensor_scalar(oh_count[:, k, :], iota_lane[:, :], s_lo[o][:, bass.ds(c, 1)], None, ALU.is_equal)
                v.tensor_scalar(oh[:, k, :], iota_f[:, 0:P], s_lo[o][:, bass.ds(c, 1)], s_w[o][:, bass.ds(c, 1)],
                                ALU.is_equal, ALU.mult).then_inc(oh_ready[o], 1)

            def add_group(o, acc, tile, g, psum, banks):
                dve.wait_ge(sum_free[o], g + banks)
                a = acc[:, bass.ds(tile, 1), :].rearrange("p t c -> p (t c)")
                v.tensor_add(a, a, psum).then_inc(sum_free[o], 1)

            def layer0(o, phase):
                def add(i, j, tile):
                    g = i * (SLOTS // GP) + j
                    dve.wait_ge(chunks_summed, i * SLOTS + (SLOTS + phase * CHUNKS + GP * j + GP))
                    add_group(o, acc[o], tile, g, bank[4 + j % 4][:, 0:HALF + 1], 4)

                def turn(i):
                    tiles = tile_numbers(mybir.EngineType.DVE, o, i * (SLOTS // GP) + (TILE_AT - 2), SLOTS // GP)
                    for k in range(SLOTS):
                        if o == "S":
                            for c in beside(k):
                                sort_column("D", i * STEP + (AHEAD * STEP + c), c % RING, PLACED["S"])
                        weighted_one_hot(o, phase, i, k)
                        j = k // GP
                        if k % GP == GP - 1 and (j >= 2 or not isinstance(i, int)):
                            add(i, j - 2, tiles[j])

                turn(0)
                with dve.Fori(1, ROUNDS) as i:
                    turn(i)
                tiles = tile_numbers(mybir.EngineType.DVE, o, TILE_AT + GROUPS - 2, 2)
                for j in range(2):
                    add(ROUNDS - 1, SLOTS // GP - 2 + j, tiles[j])
                dve.wait_ge(sum_free[o], GROUPS + 4)

            def degrees(o):
                link(v.tensor_scalar(rdeg[:, :, :], acc[o][:, :, HALF:HALF + 1], 1.0, None, ALU.max))
                link(v.reciprocal(rdeg[:, :, :], rdeg[:, :, :]))

            def add_means(o, half, a, b):
                mean = acc[o][:, a:b, 0:HALF]
                link(v.tensor_tensor(mean, mean, rdeg[:, a:b, :].to_broadcast([P, b - a, HALF]), ALU.mult))
                link(v.tensor_tensor(half[:, a:b, :], half[:, a:b, :], mean, ALU.add))

            dve.wait_ge(q_edges, 96)
            split_key(nat["src"])
            for t in range(T):
                count_tile(t)
            first_positions(0)
            for t in range(T):
                last = rank_tile(t, t % 2, 0)
            chunks_and_lanes("S", 0, last)
            make_records("S", nat["dst"])
            index_fields("S", nat["dst"])
            weight_parts()
            split_key(nat["dst"])

            dve.wait_ge(pe_chain, 1)
            for m in range(2):
                v.tensor_copy(whT[:, m, :], bank[m][:, :])
                v.tensor_copy(woT[:, 2 * m:2 * m + 2, 0:C], bank[2 + m][:, :].rearrange("p (k c) -> p k c", k=2))
            v.tensor_copy(ahT[:, :, :].rearrange("p k c -> p (k c)"), bank[4][:, 0:32])
            v.tensor_copy(woT[:, :, C:C + 2], bank[4][:, 32:40].rearrange("p (k c) -> p k c", c=2))
            v.tensor_copy(bah[0:1, :], bank[5][0:1, 0:16])
            v.tensor_copy(bao[0:1, :], bank[5][0:1, 16:18]).then_inc(w_evac, 1)

            dve.wait_ge(q_x, 32)

            def sort_by_source(i, between=None):
                for k in range(STEP):
                    if between and k * STATS % STEP == 0:
                        between(k * STATS // STEP)
                    sort_column("S", i * STEP + k, k % RING, 0)

            half = T // STATS
            with dve.Fori(0, half) as i:
                def count_and_sum(u):
                    tile_statistics(i * STATS + u)
                    count_tile(i * STATS + u)

                sort_by_source(i, count_and_sum)
            for t in range(STATS * half, T):
                tile_statistics(t)
                count_tile(t)
            for t in range(T):
                tile_moments(t, 0)
            scales(0, 0, T)
            first_positions(1)
            with dve.Fori(half, 2 * half) as i:
                sort_by_source(i, lambda u: rank_tile(i * STATS + (u - STATS * half), u % 2, T))
            for t in range(STATS * half, T):
                last = rank_tile(t, t % 2, T)
            chunks_and_lanes("D", 1, last)
            make_records("D", nat["src"])
            index_fields("D", nat["src"])
            with dve.Fori(2 * half, PLACED["S"] // STEP) as i:
                sort_by_source(i)
            merge("S", 0, PLACED["S"])

            with dve.Fori(0, AHEAD) as i:
                for k in range(STEP):
                    sort_column("D", i * STEP + k, k % RING, PLACED["S"])
            dve.wait_ge(acc_zeroed, 1)
            layer0("S", 0)
            merge("D", 1, PLACED["S"] + PLACED["D"])
            degrees("S")
            add_means("S", xs[:, :, 0:HALF], 0, T)
            dve.wait_ge(acc_zeroed, 2)
            layer0("D", 1)
            degrees("D")

            def dense(o, width, ns, s_src, landed, t):
                dve.wait_ge(dense_psum[o], t + 1)
                if t >= 2:
                    dve.wait_ge(landed[t % 2], 16 * (t // 2))
                v.tensor_tensor(stage[:, t % 2, 0:width], bank[2 + t % 2][:, 0:width], bias[o], ALU.add)
                s = bank[4 + t % 2][:, 0:2 * ns] if o == "1" else bank[2 + t % 2][:, width:width + 2]
                v.tensor_copy(s_src[:, t, :], s[:, 0:ns])
                v.tensor_copy(stage[:, t % 2, width:width + ns], s[:, ns:2 * ns]).then_inc(dense_dve[o], 1)

            dve.wait_ge(q_gains, 16 * 6)
            for b in range(T // BLOCK + 2):
                if 1 <= b <= T // BLOCK:
                    scales(b, (b - 1) * BLOCK, b * BLOCK)
                if b < T // BLOCK:
                    add_means("D", xs[:, :, HALF:C], b * BLOCK, (b + 1) * BLOCK)
                for t in range(b * BLOCK, (b + 1) * BLOCK):
                    if b < T // BLOCK:
                        tile_statistics(t)
                    if b >= 2:
                        dense("1", HD, HEADS, s_src1, tab_1, t - 2 * BLOCK)
                if b < T // BLOCK:
                    for t in range(b * BLOCK, (b + 1) * BLOCK):
                        tile_moments(t, T)

            def attend(o):
                heads, width = (HEADS, HD) if o == "1" else (1, C)
                acc = work[:, :, 0:width]
                dve.sem_inc(sum_free[o], 4)

                def scores(i, q, u):
                    n = QUAD * heads
                    dve.wait_ge(ssrc_ready[o], q + 1)
                    for k in range(QUAD):
                        b = u % UNROLL * QUAD + k
                        dve.wait_ge(gathered[b], i * 16 + 16 * ((1 + int(o)) * ROUNDS + 1 + u // UNROLL))
                    v.tensor_tensor(score[:, u % 2, 0:n].rearrange("p (k h) -> p k h", h=heads),
                                    bank[2 + u % 2][:, 0:n].rearrange("p (k h) -> p k h", h=heads),
                                    row_slots(u % UNROLL * QUAD, QUAD)[:, :, width:width + heads], ALU.add).then_inc(z_ready[o], 1)
                    dve.wait_ge(z_ready[o], q + 1)
                    v.scalar_tensor_tensor(out=lrelu[:, u % 2, 0:n], in0=score[:, u % 2, 0:n], scalar=ALPHA,
                                           in1=score[:, u % 2, 0:n], op0=ALU.mult, op1=ALU.max).then_inc(lrelu_ready[o], 1)

                def messages(q, u):
                    dve.wait_ge(e_ready[o], q + 1)
                    for k in range(QUAD):
                        row = row_slots(u * QUAD + k, 1)[:, 0, 0:width]
                        e, m = e_att[:, u % 2, k * heads:(k + 1) * heads], msg[:, u % 2 * QUAD + k, 0:width]
                        if heads == 1:
                            ins = v.tensor_scalar(m, row, e, None, ALU.mult)
                        else:
                            ins = v.tensor_tensor(m.rearrange("p (h d) -> p h d", h=heads),
                                                  row.rearrange("p (h d) -> p h d", h=heads),
                                                  e.unsqueeze(2).to_broadcast([P, heads, D]), ALU.mult)
                        ins.then_inc(msg_ready[o], 1)

                def add_groups(q, u, tiles):
                    for j in range(2):
                        dve.wait_ge(sum_ready[o], q * 2 + (j + 1))
                        add_group(o, acc, tiles[j], q * 2 + j, bank[4 + u % 2 * 2 + j][:, 0:width], 4)

                def turn(i):
                    tiles = tile_numbers(mybir.EngineType.DVE, "S", i * (2 * UNROLL) + (TILE_AT - 2), 2 * UNROLL)
                    for u in range(UNROLL):
                        q, static = i * UNROLL + u, isinstance(i, int)
                        messages(q, u)
                        if not static or q + 1 < QUADS:
                            scores(i, i * UNROLL + (u + 1), u + 1)
                        if not static or q >= 1:
                            add_groups(i * UNROLL + (u - 1), u - 1, tiles[2 * u:2 * u + 2])

                scores(0, 0, 0)
                turn(0)
                with dve.Fori(1, ROUNDS - 1) as i:
                    turn(i)
                turn(ROUNDS - 1)
                add_groups(QUADS - 1, UNROLL - 1, tile_numbers(mybir.EngineType.DVE, "S", TILE_AT + GROUPS - 2, 2))

            dve.wait_ge(acc_cleared, T)
            attend("1")
            dve.wait_ge(sum_free["1"], GROUPS + 4)

            def per_head(a):
                return a.rearrange("p (h d) -> p h d", h=HEADS)

            LAG = 3
            for t in range(T + LAG):
                if t < T:
                    link(v.tensor_reduce(head_mean[:, t, :], per_head(work[:, t, :]), AX.X, ALU.add))
                    v.tensor_scalar(head_mean[:, t, :], head_mean[:, t, :], 1.0 / D, None, ALU.mult).then_inc(head_sum, 1)
                if t >= LAG:
                    s = t - LAG
                    dve.wait_ge(squared, s + 1)
                    v.tensor_reduce(head_var[:, s, :], per_head(square[:, s % 4, :]), AX.X, ALU.add).then_inc(square_used, 1)
            dve.wait_ge(std_ready, 2 + T // BLOCK)
            link(v.reciprocal(head_var[:, :, :], head_var[:, :, :]))

            def elu(n, slot, y):
                dve.wait_ge(exp_ready, n + 1)
                return v.scalar_tensor_tensor(out=y, in0=neg_exp[:, slot, 0:y.shape[-1]], scalar=-1.0, in1=y, op0=ALU.add, op1=ALU.max)

            for t in range(T + 8):
                if t < T:
                    y = per_head(work[:, t, :])
                    v.tensor_tensor(y, y, head_var[:, t, :].unsqueeze(2).to_broadcast([P, HEADS, D]), ALU.mult).then_inc(scaled, 1)
                if 2 <= t < T + 2:
                    dve.wait_ge(gained, t - 1)
                    v.tensor_tensor(work[:, t - 2, :], work[:, t - 2, :], betah[:, :], ALU.add).then_inc(offset_added, 1)
                if 5 <= t < T + 5:
                    elu(t - 5, (t - 5) % 2, work[:, t - 5, :]).then_inc(z_done, 1)
                if t >= 8:
                    dense("2", C, 1, s_src2, tab_2, t - 8)

            dve.wait_ge(acc_cleared, 2 * T)
            attend("2")
            dve.wait_ge(sum_free["2"], GROUPS + 4)

            def finish(t):
                y = work[:, t, 0:C]
                elu(T + t, (T + t) % 2, y).then_inc(z_done, 1)
                dve.wait_ge(z_done, T + t + 1)
                if t >= 4:
                    dve.wait_ge(q_out[t % 4], 16 * (t // 4))
                v.tensor_tensor(final[:, t % 4, :], y, xs[:, t, :], ALU.add).then_inc(final_ready, 1)

            for t in range(T):
                v.bn_stats(stats[:, t, :], work[:, t, 0:C]).then_inc(stats_ready, 1)
            for t in range(T):
                tile_moments(t, 2 * T)
            dve.wait_ge(moments_ready, 3 * T)
            for t in range(T):
                v.scalar_tensor_tensor(out=work[:, t, 0:C], in0=work[:, t, 0:C], scalar=mv[:, t, 0:1], in1=go[:, :],
                                       op0=ALU.subtract, op1=ALU.mult).then_inc(gained, 1)
                if t == 0:
                    dve.wait_ge(std_ready, 3 + T // BLOCK)
                    v.reciprocal(rstd[:, :], rstd[:, :]).then_inc(nb_ready, 1)
                if t >= 6:
                    finish(t - 6)
            for t in range(T - 6, T):
                finish(t)


_INS = ["x", "src", "dst", "edge_weight", "L1_gnn_W_heads", "L1_gnn_b_heads", "L1_gnn_a_heads", "L1_gnn_g_heads",
        "L1_gnn_beta_heads", "L1_gnn_W_out", "L1_gnn_b_out", "L1_gnn_a_out", "L1_gnn_g_out", "L1_gnn_beta_out"]


def kernel(**inputs):
    import numpy as _np
    import concourse.bacc as _bacc
    from concourse import mybir as _mybir
    from concourse.bass_utils import run_bass_kernel_spmd as _run

    nc = _bacc.Bacc("TRN2", target_bir_lowering=False, num_devices=1)
    arrays, args = {}, []
    for name in _INS:
        a = _np.ascontiguousarray(inputs[name])
        arrays[f"in_{name}"] = a
        args.append(nc.dram_tensor(f"in_{name}", a.shape, _mybir.dt.from_np(a.dtype), kind="ExternalInput").ap())
    args.append(nc.dram_tensor("out_x", (N, C), _mybir.dt.float32, kind="ExternalOutput").ap())
    build(nc, *args)
    return _run(nc, [arrays], core_ids=[0]).results[0]["out_x"]
```
